# Optimizing a Trainium2 kernel written in Bass

```python
import numpy as np
import jax
import jax.numpy as jnp

def _softmax(x, axis=-1):
    return jax.nn.softmax(x, axis=axis)
def _gelu(x):
    return jax.nn.gelu(x, approximate=True)
def _silu(x):
    return jax.nn.silu(x)
def _sigmoid(x):
    return jax.nn.sigmoid(x)
def _layernorm(x, axis=-1, eps=1e-5):
    m = jnp.mean(x, axis=axis, keepdims=True)
    v = jnp.var(x, axis=axis, keepdims=True)
    return (x - m) / jnp.sqrt(v + eps)
def _scatter_add(tgt, idx, src, axis=0):
    return tgt.at[idx].add(src)
def _segment_sum(src, seg, n):
    return jax.ops.segment_sum(src, seg, n)

kernel_name = 'mk_metaformer_d1_conv_nchw256_0d2df8'

def setup_inputs(seed: int = 0):
    np.random.seed(seed)
    _w = jnp.asarray
    def _rec_inputs():
        import jax
        import jax.numpy as jnp
        _gk = jax.random.key(seed)
        x = -0.0002928 + 1 * jax.random.normal(jax.random.fold_in(_gk, 1), (4, 256, 64, 64), jnp.float32)
        return x
    x = _rec_inputs()
    def _L0_conv_setup():
        import jax, jax.numpy as jnp
        import numpy as np
        K = 3
        STRIDE = 1
        PAD = 1

        def _conv2d(x, w, b):
            y = jax.lax.conv_general_dilated(x, w, window_strides=(STRIDE, STRIDE), padding=[(PAD, PAD), (PAD, PAD)], dimension_numbers=('NCHW', 'OIHW', 'NCHW'))
            return y + b[None, :, None, None]

        def _bilinear_sample(xb, py, px):
            C, H, W = xb.shape
            y0 = jnp.floor(py)
            x0 = jnp.floor(px)
            ay = py - y0
            ax = px - x0
            out = jnp.zeros((C,) + py.shape, dtype=xb.dtype)
            corners = [(y0, x0, (1.0 - ay) * (1.0 - ax)), (y0, x0 + 1.0, (1.0 - ay) * ax), (y0 + 1.0, x0, ay * (1.0 - ax)), (y0 + 1.0, x0 + 1.0, ay * ax)]
            for yc, xc, wgt in corners:
                valid = (yc >= 0) & (yc < H) & (xc >= 0) & (xc < W)
                yi = jnp.clip(yc, 0, H - 1).astype(jnp.int32)
                xi = jnp.clip(xc, 0, W - 1).astype(jnp.int32)
                g = xb[:, yi, xi]
                out = out + g * (wgt * valid.astype(xb.dtype))[None]
            return out

        def _deform_forward(x, weight, bias, p_weight, p_bias):
            B, Cin, H, W = x.shape
            Cout = weight.shape[0]
            K2 = K * K
            pout = _conv2d(x, p_weight, p_bias)
            o1, o2, m = jnp.split(pout, 3, axis=1)
            offset = jnp.concatenate([o1, o2], axis=1)
            mask = jax.nn.sigmoid(m)
            Ho, Wo = (mask.shape[2], mask.shape[3])
            off = offset.reshape(B, K2, 2, Ho, Wo)
            dy, dx = (off[:, :, 0], off[:, :, 1])
            ki = (jnp.arange(K2) // K).astype(x.dtype)
            kj = (jnp.arange(K2) % K).astype(x.dtype)
            base_y = jnp.arange(Ho, dtype=x.dtype) * STRIDE - PAD
            base_x = jnp.arange(Wo, dtype=x.dtype) * STRIDE - PAD
            py = base_y[None, None, :, None] + ki[None, :, None, None] + dy
            px = base_x[None, None, None, :] + kj[None, :, None, None] + dx
            sampled = jax.vmap(_bilinear_sample)(x, py, px)
            sampled = sampled * mask[:, None]
            w = weight.reshape(Cout, Cin, K2)
            out = jnp.einsum('bckhw,ock->bohw', sampled, w) + bias[None, :, None, None]
            return out
        key = jax.random.key(seed)
        k1, k2, k3 = jax.random.split(key, 3)
        B, Cin, Cout, H, W = (4, 256, 256, 64, 64)
        x = jax.random.normal(k1, (B, Cin, H, W), dtype=jnp.float32)
        fan_in = Cin * K * K
        weight = jax.random.normal(k2, (Cout, Cin, K, K), dtype=jnp.float32) / np.sqrt(fan_in)
        bias = jnp.zeros((Cout,), dtype=jnp.float32)
        p_weight = jax.random.normal(k3, (3 * K * K, Cin, K, K), dtype=jnp.float32) * 0.02
        p_bias = jnp.zeros((3 * K * K,), dtype=jnp.float32)
        return {'x': x, 'weight': weight, 'bias': bias, 'p_weight': p_weight, 'p_bias': p_bias}
    _L0_conv_all = _L0_conv_setup()
    _L0_conv_in = {k: v for k, v in _L0_conv_all.items() if k in ('weight', 'bias', 'p_weight', 'p_bias', )}
    del _L0_conv_all

    def _L0_ffn_setup():
        import jax, jax.numpy as jnp
        import numpy as np
        NUM_EXPERTS = 8
        TOP_K = 2
        B, S, D = (8, 8192, 256)

        def _moe(tokens, router_w, w1, b1, w2, b2):
            N = tokens.shape[0]
            E = router_w.shape[0]
            logits = tokens.astype(jnp.float32) @ router_w.astype(jnp.float32).T
            probs = jax.nn.softmax(logits, axis=-1)
            rw, re = jax.lax.top_k(probs, TOP_K)
            if TOP_K > 1:
                rw = rw / jnp.maximum(rw.sum(-1, keepdims=True), 1e-12)
            rw = rw.astype(tokens.dtype)
            combine = jnp.zeros((N, E), tokens.dtype).at[jnp.arange(N)[:, None], re].set(rw)
            out = tokens
            for e in range(E):
                h = jax.nn.gelu(tokens @ w1[e] + b1[e], approximate=False)
                y = h @ w2[e] + b2[e]
                out = out + combine[:, e:e + 1] * y
            return out
        key = jax.random.key(seed)
        ks = jax.random.split(key, 4)
        scale = 1.0 / np.sqrt(D).astype(np.float32)
        return {'input_embeddings': jax.random.normal(ks[0], (B, S, D), jnp.float32), 'router_w': jax.random.normal(ks[1], (NUM_EXPERTS, D), jnp.float32) * scale, 'w1': jax.random.normal(ks[2], (NUM_EXPERTS, D, D), jnp.float32) * scale, 'b1': jnp.zeros((NUM_EXPERTS, D), jnp.float32), 'w2': jax.random.normal(ks[3], (NUM_EXPERTS, D, D), jnp.float32) * scale, 'b2': jnp.zeros((NUM_EXPERTS, D), jnp.float32)}
    _L0_ffn_all = _L0_ffn_setup()
    _L0_ffn_in = {k: v for k, v in _L0_ffn_all.items() if k in ('router_w', 'w1', 'b1', 'w2', 'b2', )}
    del _L0_ffn_all

    return {
        "x": x,
        "L0_conv_weight": _L0_conv_in["weight"],
        "L0_conv_bias": _L0_conv_in["bias"],
        "L0_conv_p_weight": _L0_conv_in["p_weight"],
        "L0_conv_p_bias": _L0_conv_in["p_bias"],
        "L0_ffn_router_w": _L0_ffn_in["router_w"],
        "L0_ffn_w1": _L0_ffn_in["w1"],
        "L0_ffn_b1": _L0_ffn_in["b1"],
        "L0_ffn_w2": _L0_ffn_in["w2"],
        "L0_ffn_b2": _L0_ffn_in["b2"],
    }

def reference(x, L0_conv_weight, L0_conv_bias, L0_conv_p_weight, L0_conv_p_bias, L0_ffn_router_w, L0_ffn_w1, L0_ffn_b1, L0_ffn_w2, L0_ffn_b2):
    import jax
    import jax.numpy as jnp
    def _L0_conv_ref(x, weight, bias, p_weight, p_bias):
        import jax, jax.numpy as jnp
        import numpy as np
        K = 3
        STRIDE = 1
        PAD = 1

        def _conv2d(x, w, b):
            y = jax.lax.conv_general_dilated(x, w, window_strides=(STRIDE, STRIDE), padding=[(PAD, PAD), (PAD, PAD)], dimension_numbers=('NCHW', 'OIHW', 'NCHW'))
            return y + b[None, :, None, None]

        def _bilinear_sample(xb, py, px):
            C, H, W = xb.shape
            y0 = jnp.floor(py)
            x0 = jnp.floor(px)
            ay = py - y0
            ax = px - x0
            out = jnp.zeros((C,) + py.shape, dtype=xb.dtype)
            corners = [(y0, x0, (1.0 - ay) * (1.0 - ax)), (y0, x0 + 1.0, (1.0 - ay) * ax), (y0 + 1.0, x0, ay * (1.0 - ax)), (y0 + 1.0, x0 + 1.0, ay * ax)]
            for yc, xc, wgt in corners:
                valid = (yc >= 0) & (yc < H) & (xc >= 0) & (xc < W)
                yi = jnp.clip(yc, 0, H - 1).astype(jnp.int32)
                xi = jnp.clip(xc, 0, W - 1).astype(jnp.int32)
                g = xb[:, yi, xi]
                out = out + g * (wgt * valid.astype(xb.dtype))[None]
            return out

        def _deform_forward(x, weight, bias, p_weight, p_bias):
            B, Cin, H, W = x.shape
            Cout = weight.shape[0]
            K2 = K * K
            pout = _conv2d(x, p_weight, p_bias)
            o1, o2, m = jnp.split(pout, 3, axis=1)
            offset = jnp.concatenate([o1, o2], axis=1)
            mask = jax.nn.sigmoid(m)
            Ho, Wo = (mask.shape[2], mask.shape[3])
            off = offset.reshape(B, K2, 2, Ho, Wo)
            dy, dx = (off[:, :, 0], off[:, :, 1])
            ki = (jnp.arange(K2) // K).astype(x.dtype)
            kj = (jnp.arange(K2) % K).astype(x.dtype)
            base_y = jnp.arange(Ho, dtype=x.dtype) * STRIDE - PAD
            base_x = jnp.arange(Wo, dtype=x.dtype) * STRIDE - PAD
            py = base_y[None, None, :, None] + ki[None, :, None, None] + dy
            px = base_x[None, None, None, :] + kj[None, :, None, None] + dx
            sampled = jax.vmap(_bilinear_sample)(x, py, px)
            sampled = sampled * mask[:, None]
            w = weight.reshape(Cout, Cin, K2)
            out = jnp.einsum('bckhw,ock->bohw', sampled, w) + bias[None, :, None, None]
            return out
        return _deform_forward(x, weight, bias, p_weight, p_bias)

    def _L0_ffn_ref(input_embeddings, router_w, w1, b1, w2, b2):
        import jax, jax.numpy as jnp
        import numpy as np
        NUM_EXPERTS = 8
        TOP_K = 2
        B, S, D = (8, 8192, 256)

        def _moe(tokens, router_w, w1, b1, w2, b2):
            N = tokens.shape[0]
            E = router_w.shape[0]
            logits = tokens.astype(jnp.float32) @ router_w.astype(jnp.float32).T
            probs = jax.nn.softmax(logits, axis=-1)
            rw, re = jax.lax.top_k(probs, TOP_K)
            if TOP_K > 1:
                rw = rw / jnp.maximum(rw.sum(-1, keepdims=True), 1e-12)
            rw = rw.astype(tokens.dtype)
            combine = jnp.zeros((N, E), tokens.dtype).at[jnp.arange(N)[:, None], re].set(rw)
            out = tokens
            for e in range(E):
                h = jax.nn.gelu(tokens @ w1[e] + b1[e], approximate=False)
                y = h @ w2[e] + b2[e]
                out = out + combine[:, e:e + 1] * y
            return out
        b, s, d = input_embeddings.shape
        tokens = input_embeddings.reshape(b * s, d)
        return _moe(tokens, router_w, w1, b1, w2, b2).reshape(b, s, d)

    def _gn(v, G=32, eps=1e-5):
        B_, C_, H_, W_ = v.shape
        g = v.reshape(B_, G, C_ // G, H_, W_)
        m = jnp.mean(g, axis=(2, 3, 4), keepdims=True)
        s = jnp.var(g, axis=(2, 3, 4), keepdims=True)
        return ((g - m) / jnp.sqrt(s + eps)).reshape(v.shape)

    def _ln_c(v, eps=1e-6):
        m = jnp.mean(v, axis=1, keepdims=True)
        s = jnp.var(v, axis=1, keepdims=True)
        return (v - m) / jnp.sqrt(s + eps)

    def _ln_t(v, eps=1e-5):
        m = jnp.mean(v, axis=-1, keepdims=True)
        s = jnp.var(v, axis=-1, keepdims=True)
        return (v - m) / jnp.sqrt(s + eps)

    def _to_tokens(v):
        B_, C_, H_, W_ = v.shape
        return v.reshape(B_, C_, H_ * W_).transpose(0, 2, 1)
    def _from_tokens(t, like):
        B_, C_, H_, W_ = like.shape
        return t.transpose(0, 2, 1).reshape(B_, C_, H_, W_)

    x = x + _L0_conv_ref(_ln_c(x), L0_conv_weight, L0_conv_bias, L0_conv_p_weight, L0_conv_p_bias)
    t = _to_tokens(x)
    t = t + _L0_ffn_ref(_ln_t(t), L0_ffn_router_w, L0_ffn_w1, L0_ffn_b1, L0_ffn_w2, L0_ffn_b2)
    x = _from_tokens(t, x)
    return x


_drawn_inputs = setup_inputs


def setup_inputs(seed=0):
    import zlib

    import numpy as np

    out = dict(_drawn_inputs(seed))
    spreads = {'L0_conv_bias': (0.0, 0.1),
     'L0_conv_p_bias': (0.0, 0.1),
     'L0_ffn_b1': (0.0, 0.336),
     'L0_ffn_b2': (0.0, 0.1)}
    factors = {}
    for name, (base, spread) in spreads.items():
        noise = np.random.default_rng([zlib.crc32(name.encode()), seed]).standard_normal(out[name].shape)
        drawn = base * np.exp(spread * noise) if base else spread * noise
        out[name] = jnp.asarray(drawn.astype(out[name].dtype))
    for name, factor in factors.items():
        out[name] = (out[name] * factor).astype(out[name].dtype)
    return out
```

```python
from contextlib import ExitStack

import concourse.bass as bass
from concourse import mybir

F32 = mybir.dt.float32
I32 = mybir.dt.int32
ALU = mybir.AluOpType
ACT = mybir.ActivationFunctionType
AX = mybir.AxisListType.X

PT = 128
C = 256
CC = C // PT
HW = 64
TILES = 4
GT = TILES * PT
ROWS = GT // HW
GPI = HW // ROWS
TAPS = 9
OFF = 3 * TAPS
TW = HW + 2
TH = HW + 1
ENT = 2 * C
SAMP = TILES * TAPS
PAIRS = SAMP // 2
GRING = 6
SRING = 6
TRING = 3
E = 8
LN_C_EPS, LN_T_EPS = 1e-6, 1e-5
RING = 16
LAG_P, LAG_B, LAG_M, LAG_O = 1, 9, 10, 11


def build(nc, groups, xg, conv_w, conv_b, off_w, off_b, router_w, w1, b1, w2, b2,
          ident_c, stack_c, tapy_c, tapx_c, rowbase_c, idxbase_c, rev_c, out):
    images = groups // GPI
    table = nc.dram_tensor("patch_table", (images * TH * TW, ENT), F32, kind="Internal").ap()

    ctx = ExitStack()
    with ctx:
        def sb(name, shape, dt=F32):
            return ctx.enter_context(nc.sbuf_tensor(name, shape, dt))

        def bank(name, shape):
            return ctx.enter_context(nc.psum_tensor(name, shape, F32))

        def sem(name):
            return ctx.enter_context(nc.semaphore(name))

        convw = sb("convw", [PT, TAPS, CC, C])
        convb = sb("convb", [PT, C])
        offw = sb("offw", [PT, CC, 3, 3, 32])
        offb = sb("offb", [PT, TILES, OFF])
        rw = sb("rw", [PT, CC, E])
        w1s = sb("w1s", [PT, E, CC, C])
        w2s = sb("w2s", [PT, E, CC, C])
        b1s = sb("b1s", [PT, E, CC])
        b2s = sb("b2s", [E, C])
        ident = sb("ident", [PT, PT])
        stack = sb("stack", [96, OFF])
        tapy = sb("tapy", [PT, SAMP])
        tapx = sb("tapx", [PT, SAMP])
        rowbase = sb("rowbase", [PT, groups])
        idxbase = sb("idxbase", [PT, groups])
        rev = sb("rev", [PT, TILES, E])
        minus_half = sb("minus_half", [PT, TILES])
        zeros = sb("zeros", [PT, ENT])
        xa = sb("xa", [PT, CC, GT])
        xn = sb("xn", [PT, TILES, C])
        chan = sb("chan", [PT, CC, HW + 2, HW])
        st_a = sb("st_a", [PT, TILES, 6])
        mv_a = sb("mv_a", [PT, TILES, 2])
        ve_a = sb("ve_a", [PT, TILES])
        rs_a = sb("rs_a", [PT, TILES])
        shifted = sb("shifted", [96, ROWS, HW])
        po = sb("po", [PT, TILES, OFF])
        pos = sb("pos", [PT, 2, SAMP])
        cell_i = sb("cell_i", [PT, 2, SAMP], I32)
        cell = sb("cell", [PT, 2, SAMP])
        over = sb("over", [PT, 2, SAMP])
        hi_w = sb("hi_w", [PT, 2, SAMP])
        lo_w = sb("lo_w", [PT, 2, SAMP])
        mask = sb("mask", [PT, SAMP])
        my = sb("my", [PT, 2, SAMP])
        flat = sb("flat", [PT, SAMP])
        idx_ring = sb("idx_ring", [PT, RING, SAMP], I32)
        w_ring = sb("w_ring", [PT, RING, 4, SAMP])
        idx = sb("idx", [PT, SAMP], I32)
        w_act = sb("w_act", [PT, SAMP])
        w_dve = sb("w_dve", [PT, 3, SAMP])
        patch = sb("patch", [PT, GRING, 4 * C])
        samp = sb("samp", [PT, SRING, C])
        sampT = sb("sampT", [PT, TRING, 2, CC, PT])
        xb = sb("xb", [PT, CC, GT])
        x1 = sb("x1", [PT, TILES, C])
        z = sb("z", [PT, TILES, C])
        st_b = sb("st_b", [PT, 6])
        mv_b = sb("mv_b", [PT, 2])
        ve_b = sb("ve_b", [PT, 1])
        rs_b = sb("rs_b", [PT, 1])
        zT = sb("zT", [PT, CC, GT])
        lg = sb("lg", [PT, TILES, E])
        lg2 = sb("lg2", [PT, TILES, E])
        cand = sb("cand", [PT, TILES, E])
        hot1 = sb("hot1", [PT, TILES, E])
        hot2 = sb("hot2", [PT, TILES, E])
        ex = sb("ex", [PT, TILES, E])
        red = sb("red", [PT, 6, TILES])
        comb = sb("comb", [PT, TILES, E])
        combT = sb("combT", [E, TILES, PT])
        hT = sb("hT", [PT, 2, CC, GT])
        acc = sb("acc", [PT, TILES, C])
        outT = sb("outT", [PT, CC, GT])

        ps_t = [bank(f"ps_t{i}", [PT, 2, CC, PT]) for i in range(2)]
        ps_conv = [bank(f"ps_conv{i}", [PT, GT]) for i in range(2)]
        ps_m = bank("ps_m", [PT, GT])
        ps_h = bank("ps_h", [PT, GT])
        ps_y = [bank(f"ps_y{i}", [PT, GT]) for i in range(2)]

        s_ident = sem("s_ident")
        s_const = sem("s_const")
        s_zero = sem("s_zero")
        s_offw0 = sem("s_offw0")
        s_pad = sem("s_pad")
        s_xa = sem("s_xa")
        s_xb = sem("s_xb")
        s_tab = sem("s_tab")
        s_out = sem("s_out")
        s_patch = [sem(f"s_patch{i}") for i in range(GRING)]
        s_idx = sem("s_idx")
        s_a_tok = sem("s_a_tok")
        s_a_raw = sem("s_a_raw")
        s_a_norm = sem("s_a_norm")
        s_a_back = sem("s_a_back")
        s_a_rows = sem("s_a_rows")
        s_p_conv = sem("s_p_conv")
        s_p_shift = sem("s_p_shift")
        s_p_off = sem("s_p_off")
        s_p_po = sem("s_p_po")
        s_p_tanh = sem("s_p_tanh")
        s_p_done = sem("s_p_done")
        s_wact = sem("s_wact")
        s_first = sem("s_first")
        s_samp = sem("s_samp")
        s_trans = sem("s_trans")
        s_sampT = sem("s_sampT")
        s_conv = sem("s_conv")
        s_x1 = sem("s_x1")
        s_z = sem("s_z")
        s_xb_used = sem("s_xb_used")
        s_zt_t = sem("s_zt_t")
        s_zt = sem("s_zt")
        s_logit = sem("s_logit")
        s_lg = sem("s_lg")
        s_ex = sem("s_ex")
        s_comb = sem("s_comb")
        s_ct_t = sem("s_ct_t")
        s_ct = sem("s_ct")
        s_h = sem("s_h")
        s_g = sem("s_g")
        s_y = sem("s_y")
        s_acc = sem("s_acc")
        s_o_t = sem("s_o_t")
        s_o = sem("s_o")
        s_var_a = sem("s_var_a")
        s_rstd_a = sem("s_rstd_a")
        s_var = sem("s_var")
        s_rstd = sem("s_rstd")
        s_ve = sem("s_ve")
        s_ve_a = sem("s_ve_a")
        s_wdve = sem("s_wdve")
        s_acc0 = sem("s_acc0")
        s_seen_dve = sem("s_seen_dve")
        s_seen_pool = sem("s_seen_pool")
        s_st_a = sem("s_st_a")
        s_place = sem("s_place")
        s_blend = sem("s_blend")
        s_fin = sem("s_fin")
        s_top = sem("s_top")
        YUSES = TILES * (E + 1)
        YM = TILES * E

        CONSTS = [(convw, conv_w), (convb, conv_b.partition_broadcast(PT)), (rw, router_w), (w1s, w1), (w2s, w2),
                  (b1s, b1), (b2s, b2), (stack, stack_c), (tapy, tapy_c), (tapx, tapx_c),
                  (rowbase, rowbase_c), (idxbase, idxbase_c), (rev, rev_c)]
        N_CONST = len(CONSTS) + CC * 3 + TILES
        N_PAD = 4 + images - 1

        last = groups + LAG_O
        cuts = sorted({0, 1, 2, GPI, LAG_B, LAG_B + 1, LAG_B + 2, LAG_B + 3, groups, groups + 1, groups + LAG_B,
                       groups + LAG_B + 1, last})
        segments = [(a, b) for a, b in zip(cuts, cuts[1:])]

        def active(i):
            return {s: 0 <= i - lag < groups
                    for s, lag in (("A", 0), ("P", LAG_P), ("B", LAG_B), ("M", LAG_M), ("O", LAG_O))}

        def iterate(eng, body):
            for lo, hi in segments:
                if hi - lo == 1:
                    body(lo, active(lo))
                else:
                    with eng.Fori(lo, hi) as i:
                        body(i, active(lo))

        def count(value):
            return max(value, 0) if isinstance(value, int) else value

        def tile_of(s):
            return s // TAPS, s % TAPS

        ends_at = {(TAPS * t + TAPS - 1) // 2: t for t in range(TILES)}

        block = ctx.enter_context(nc.Block())

        @block.sync
        def _(sp):
            sp.dma_start(ident[:], ident_c).then_inc(s_ident, 16)
            for dst, src in CONSTS:
                sp.dma_start(dst[:], src).then_inc(s_const, 16)
            sp.wait_ge(s_offw0, 1)
            for cc in range(CC):
                for ky in range(3):
                    sp.dma_start(offw[:, cc, ky, :, 0:OFF], off_w[:, cc, ky]).then_inc(s_const, 16)
            for t in range(TILES):
                sp.dma_start(offb[:, t], off_b.partition_broadcast(PT)).then_inc(s_const, 16)
            sp.wait_ge(s_zero, 1)
            first = table[0:TH * TW].rearrange("(y x) e -> y x e", x=TW)
            sp.dma_start(first[0, 1:HW + 1, 0:C], zeros[0:HW, 0:C]).then_inc(s_pad, 16)
            sp.dma_start(first[HW, 1:HW + 1, C:ENT], zeros[0:HW, 0:C]).then_inc(s_pad, 16)
            sp.dma_start(first[:, 0, :], zeros[0:TH, :]).then_inc(s_pad, 16)
            sp.dma_start(first[:, TW - 1, :], zeros[0:TH, :]).then_inc(s_pad, 16)
            for b in range(1, images):
                rest = table[b * TH * TW:(b + 1) * TH * TW].rearrange("(x y) e -> x y e", x=TW)
                sp.dma_start(rest, zeros[0:TW].unsqueeze(1).broadcast_to([TW, TH, ENT])).then_inc(s_pad, 16)

            def body(i, on):
                a = i
                if isinstance(i, int) and i == GPI:
                    sp.wait_ge(s_pad, 16 * N_PAD)
                if on["A"]:
                    sp.wait_ge(s_a_tok, count(2 * a))
                    sp.dma_start(xa[:], xg[a]).then_inc(s_xa, 16)
                    sp.wait_ge(s_a_norm, a + 1)
                    entries = table.rearrange("(y x) e -> y x e", x=TW)
                    for half in range(2):
                        for r in range(2):
                            y = a * ROWS + a // GPI + (r + 1 - half)
                            dst = entries[bass.ds(y, TILES, 2), 1:HW + 1, half * C:(half + 1) * C]
                            sp.dma_start(dst.rearrange("t x c -> x t c"),
                                         xn[HW * r:HW * r + HW]).then_inc(s_tab, 16)
                if on["O"]:
                    o = i - LAG_O
                    sp.wait_ge(s_o, CC * o + CC)
                    sp.dma_start(out[o], outT[:]).then_inc(s_out, 16)

            iterate(sp, body)
            sp.wait_ge(s_out, 16 * groups)
            sp.wait_ge(s_tab, 64 * groups)
            sp.wait_ge(s_pad, 16 * N_PAD)

        @block.gpsimd
        def _(pool):
            nc.gpsimd.memset(zeros[:], 0.0).then_inc(s_zero, 1)
            nc.gpsimd.memset(minus_half[:], -0.5)
            nc.gpsimd.memset(offw[:], 0.0).then_inc(s_offw0, 1)
            nc.gpsimd.memset(shifted[:], 0.0)
            nc.gpsimd.memset(chan[:, :, 0:1], 0.0)
            nc.gpsimd.memset(chan[:, :, HW + 1:HW + 2], 0.0).then_inc(s_zero, 1)

            def body(i, on):
                a, g, m = i, i - LAG_B, i - LAG_M

                def rsqrt_tile(t, gg):
                    pool.wait_ge(s_var, TILES * gg + t + 1)
                    pool.wait_ge(s_z, count(TILES * gg + t))
                    pool.sem_inc(s_seen_pool, 1)
                    nc.gpsimd.tensor_scalar(ve_b[:], mv_b[:, 1:2], LN_T_EPS, None, ALU.add).then_inc(s_ve, 1)
                    pool.wait_ge(s_ve, TILES * gg + t + 1)
                    nc.gpsimd.tensor_tensor(rs_b[:], ve_b[:], minus_half[:, 0:1], ALU.pow).then_inc(s_rstd, 1)

                def rsqrt_channels():
                    pool.wait_ge(s_var_a, a + 1)
                    pool.wait_ge(s_a_norm, count(a))
                    pool.sem_inc(s_seen_pool, 1)
                    nc.gpsimd.tensor_scalar(ve_a[:], mv_a[:, :, 1], LN_C_EPS, None, ALU.add).then_inc(s_ve_a, 1)
                    pool.wait_ge(s_ve_a, a + 1)
                    nc.gpsimd.tensor_tensor(rs_a[:], ve_a[:], minus_half[:], ALU.pow).then_inc(s_rstd_a, 1)

                if not on["B"]:
                    if on["M"]:
                        rsqrt_tile(TILES - 1, m)
                    if on["A"]:
                        rsqrt_channels()
                    return
                pool.wait_ge(s_p_done, g + 1)
                for slot in range(GRING):
                    pool.wait_ge(s_patch[slot], count(16 * (SAMP // GRING) * g))
                nc.gpsimd.tensor_copy(idx[:], idx_ring[:, g % RING]).then_inc(s_idx, 1)
                pool.wait_ge(s_idx, g + 1)
                pool.wait_ge(s_tab, count(64 * GPI * (g // GPI) + 64 * GPI))
                pool.wait_ge(s_xb_used, count(g))
                pool.dma_start(xb[:], xg[g]).then_inc(s_xb, 16)
                for s in range(SAMP):
                    pool.wait_ge(s_pad, 16 * N_PAD)
                    pool.wait_ge(s_samp, count(SAMP * g + s - GRING + 1))
                    pool.sem_inc(s_seen_pool, 1)
                    nc.gpsimd.indirect_dma_start(
                        patch[:, s % GRING], None, table,
                        bass.IndirectOffsetOnAxis(idx[:, s:s + 1], 0)).then_inc(s_patch[s % GRING], 16)
                    if s == 7 and on["M"]:
                        rsqrt_tile(TILES - 1, m)
                    if s == 13 and on["A"]:
                        rsqrt_channels()
                    if s in (19, 27, 35):
                        rsqrt_tile((19, 27, 35).index(s), g)

            iterate(pool, body)

        @block.scalar
        def _(act):
            act.wait_ge(s_zero, 2)

            def body(i, on):
                a, p, g, m, o = i, i - LAG_P, i - LAG_B, i - LAG_M, i - LAG_O

                if isinstance(i, int) and i == LAG_P:
                    act.wait_ge(s_const, 16 * N_CONST)

                def first_corner(j):
                    for s in (2 * j, 2 * j + 1):
                        act.wait_ge(s_patch[s % GRING], 16 * (SAMP // GRING) * g + 16 * (s // GRING) + 16)
                        act.wait_ge(s_trans, count(PAIRS * g + j - SRING // 2 + 1))
                        nc.scalar.activation(samp[:, s % SRING], patch[:, s % GRING, 0:C], ACT.Copy,
                                             scale=w_act[:, s:s + 1]).then_inc(s_first, 1)

                def keep_pair(j):
                    act.wait_ge(s_trans, PAIRS * g + j + 1)
                    act.wait_ge(s_conv, count(PAIRS * g + j - TRING + 1))
                    nc.scalar.copy(sampT[:, j % TRING], ps_t[j % 2][:]).then_inc(s_sampT, 1)

                def gelu(e, fc):
                    act.wait_ge(s_h, CC * E * m + CC * e + fc + 1)
                    act.wait_ge(s_y, count(YUSES * m + TILES * e if e >= 2 else YUSES * (m - 1) + TILES * (E + e)))
                    nc.scalar.activation(hT[:, e % 2, fc], ps_h[:], ACT.Gelu,
                                         bias=b1s[:, e, fc:fc + 1]).then_inc(s_g, 1)

                if on["B"]:
                    act.wait_ge(s_p_done, g + 1)
                    act.wait_ge(s_first, count(SAMP * g))
                    nc.scalar.copy(w_act[:], w_ring[:, g % RING, 0]).then_inc(s_wact, 1)
                    act.wait_ge(s_wact, g + 1)
                    first_corner(0)
                for j in range(PAIRS):
                    first_half = j >= 3 and j % 2 == 1 and on["M"]
                    if on["B"] and j + 1 < PAIRS:
                        first_corner(j + 1)
                    if first_half:
                        gelu((j - 3) // 2, 0)
                    if on["B"]:
                        keep_pair(j)
                    if first_half:
                        gelu((j - 3) // 2, 1)
                    if j in (0, 2) and on["A"]:
                        q = j // 2
                        act.wait_ge(s_a_tok, 2 * a + q + 1)
                        act.wait_ge(s_tab, count(64 * a))
                        act.wait_ge(s_a_back, count(2 * a))
                        nc.scalar.copy(xn[:, 2 * q:2 * q + 2].rearrange("p t c -> p (t c)"),
                                       ps_m[:]).then_inc(s_a_raw, 1)
                    if j == 1 and on["M"]:
                        for cc in range(CC):
                            act.wait_ge(s_zt_t, CC * m + cc + 1)
                            act.wait_ge(s_h, count(CC * E * m))
                            nc.scalar.copy(zT[:, cc], (ps_h, ps_m)[cc][:]).then_inc(s_zt, 1)
                    if j in (3, 4) and on["O"]:
                        cc = j - 3
                        act.wait_ge(s_out, count(16 * o))
                        act.wait_ge(s_o_t, CC * o + cc + 1)
                        nc.scalar.copy(outT[:, cc], ps_m[:]).then_inc(s_o, 1)
                    if j == 3 and on["M"]:
                        act.wait_ge(s_lg, m + 1)
                        nc.scalar.activation(ex[:], ex[:], ACT.Exp).then_inc(s_ex, 1)
                    if j in (5, 6) and on["A"]:
                        q = j - 5
                        act.wait_ge(s_a_back, 2 * a + q + 1)
                        act.wait_ge(s_p_conv, count(a - 1))
                        row = (a % GPI) * ROWS + 1 + 4 * q
                        dst = chan[:, :, bass.ds(row, 4), :].rearrange("p c r w -> p c (r w)")
                        nc.scalar.copy(dst, ps_m[:].rearrange("p (c n) -> p c n", c=CC)).then_inc(s_a_rows, 1)
                    if j == 8 and on["P"]:
                        act.wait_ge(s_p_conv, p + 1)
                        act.wait_ge(s_p_off, count(p))
                        ps = ps_m[:].rearrange("p (r w) -> p r w", w=HW)
                        nc.scalar.copy(shifted[0:32, :, 1:HW], ps[0:32, :, 0:HW - 1])
                        nc.scalar.copy(shifted[32:64, :, :], ps[32:64, :, :])
                        nc.scalar.copy(shifted[64:96, :, 0:HW - 1], ps[64:96, :, 1:HW]).then_inc(s_p_shift, 1)
                    if j == 11 and on["P"]:
                        act.wait_ge(s_p_po, p + 1)
                        act.wait_ge(s_p_done, count(p))
                        nc.scalar.activation(mask[:].rearrange("p (t k) -> p t k", t=TILES), po[:, :, 2 * TAPS:OFF],
                                             ACT.Tanh, scale=0.5).then_inc(s_p_tanh, 1)

            iterate(act, body)

        @block.vector
        def _(dve):

            def body(i, on):
                a, p, g, m, o = i, i - LAG_P, i - LAG_B, i - LAG_M, i - LAG_O
                if isinstance(i, int) and i == LAG_P:
                    dve.wait_ge(s_const, 16 * N_CONST)

                def chain(semaphore, per_group, group, done=0):
                    links = [done]

                    def link(ins):
                        links[0] += 1
                        assert links[0] <= per_group
                        ins.then_inc(semaphore, 1)
                        dve.wait_ge(semaphore, count(per_group * group + links[0]))
                    return link

                def blend(j):
                    pair = (2 * j, 2 * j + 1)
                    for c in range(1, 4):
                        for s in pair:
                            src = patch[:, s % GRING, c * C:(c + 1) * C]
                            if c == 1:
                                dve.wait_ge(s_patch[s % GRING], 16 * (SAMP // GRING) * g + 16 * (s // GRING) + 16)
                                dve.wait_ge(s_first, SAMP * g + s + 1)
                            else:
                                dve.wait_ge(s_blend, count(2 * SAMP * g + 4 * j + 2 * (c - 2) + (s % 2) + 1))
                            ins = nc.vector.scalar_tensor_tensor(
                                samp[:, s % SRING], src, w_dve[:, c - 1, s:s + 1], samp[:, s % SRING],
                                ALU.mult, ALU.add)
                            ins.then_inc(s_samp if c == 3 else s_blend, 1)

                def finish_tile(t, gg):
                    dve.wait_ge(s_conv, count(PAIRS * gg + (TAPS * t + TAPS - 1) // 2 + 1))
                    ins = nc.vector.tensor_tensor(x1[:, t], ps_conv[t % 2][:, 0:C], convb[:], ALU.add)
                    ins.then_inc(s_x1, 1)
                    dve.wait_ge(s_x1, TILES * gg + t + 1)
                    nc.vector.bn_stats(st_b[:], x1[:, t]).then_inc(s_fin, 1)
                    dve.wait_ge(s_fin, TILES * gg + t + 1)
                    dve.sem_inc(s_seen_dve, 1)
                    nc.vector.bn_aggr(mv_b[:], st_b[:]).then_inc(s_var, 1)

                def norm_tile(t, gg):
                    dve.wait_ge(s_var, TILES * gg + t + 1)
                    dve.wait_ge(s_rstd, TILES * gg + t + 1)
                    dve.wait_ge(s_zt_t, count(CC * gg))
                    nc.vector.tensor_scalar(z[:, t], x1[:, t], mv_b[:, 0:1], rs_b[:], ALU.subtract,
                                            ALU.mult).then_inc(s_z, 1)
                    dve.wait_ge(s_z, TILES * gg + t + 1)

                def add_expert(e, mm):
                    for t in range(TILES):
                        use = TILES * (e + 1) + t
                        dve.wait_ge(s_y, YUSES * mm + use + 1)
                        dve.wait_ge(s_acc, count(YUSES * mm + use - TILES + 1))
                        nc.vector.scalar_tensor_tensor(acc[:, t], ps_y[use % 2][:, 0:C], comb[:, t, e:e + 1], acc[:, t],
                                                       ALU.mult, ALU.add).then_inc(s_acc, 1)

                def channel_stats():
                    dve.wait_ge(s_a_raw, 2 * a + 2)
                    for t in range(TILES):
                        ins = nc.vector.bn_stats(st_a[:, t], xn[:, t])
                    ins.then_inc(s_st_a, 1)
                    dve.wait_ge(s_st_a, a + 1)
                    dve.sem_inc(s_seen_dve, 1)
                    for t in range(TILES):
                        ins = nc.vector.bn_aggr(mv_a[:, t], st_a[:, t])
                    ins.then_inc(s_var_a, 1)

                def norm_channels():
                    dve.wait_ge(s_var_a, a + 1)
                    dve.wait_ge(s_rstd_a, a + 1)
                    for t in range(TILES):
                        ins = nc.vector.tensor_scalar(xn[:, t], xn[:, t], mv_a[:, t, 0:1], rs_a[:, t:t + 1],
                                                      ALU.subtract, ALU.mult)
                    ins.then_inc(s_a_norm, 1)

                def top2():
                    then = chain(s_top, 20, m)
                    dve.wait_ge(s_logit, m + 1)
                    dve.wait_ge(s_acc, count(YUSES * m))
                    then(nc.vector.tensor_copy(lg[:], ps_y[0][:, 0:TILES * E].rearrange("p (t e) -> p t e", e=E)))

                    def over_experts(r):
                        return red[:, r].unsqueeze(2).broadcast_to([PT, TILES, E])

                    then(nc.vector.tensor_reduce(red[:, 0], lg[:], AX, ALU.max))
                    nc.vector.tensor_tensor(ex[:], lg[:], over_experts(0), ALU.subtract).then_inc(s_lg, 1)
                    then(nc.vector.tensor_tensor(cand[:], lg[:], over_experts(0), ALU.is_equal))
                    then(nc.vector.tensor_tensor(cand[:], cand[:], rev[:], ALU.mult))
                    then(nc.vector.tensor_reduce(red[:, 1], cand[:], AX, ALU.max))
                    then(nc.vector.tensor_tensor(hot1[:], cand[:], over_experts(1), ALU.is_equal))
                    then(nc.vector.scalar_tensor_tensor(lg2[:], hot1[:], -3.0e38, lg[:], ALU.mult, ALU.add))
                    then(nc.vector.tensor_reduce(red[:, 1], lg2[:], AX, ALU.max))
                    then(nc.vector.tensor_tensor(cand[:], lg2[:], over_experts(1), ALU.is_equal))
                    then(nc.vector.tensor_tensor(cand[:], cand[:], rev[:], ALU.mult))
                    then(nc.vector.tensor_reduce(red[:, 1], cand[:], AX, ALU.max))
                    then(nc.vector.tensor_tensor(hot2[:], cand[:], over_experts(1), ALU.is_equal))
                    then(nc.vector.tensor_tensor(hot1[:], hot1[:], hot2[:], ALU.add))
                    dve.wait_ge(s_ex, m + 1)
                    then(nc.vector.tensor_reduce(red[:, 2], ex[:], AX, ALU.add))
                    then(nc.vector.reciprocal(red[:, 2], red[:, 2]))
                    then(nc.vector.tensor_tensor(ex[:], ex[:], over_experts(2), ALU.mult))
                    then(nc.vector.tensor_tensor(ex[:], ex[:], hot1[:], ALU.mult))
                    then(nc.vector.tensor_reduce(red[:, 3], ex[:], AX, ALU.add))
                    then(nc.vector.tensor_scalar(red[:, 3], red[:, 3], 1e-12, None, ALU.max))
                    then(nc.vector.reciprocal(red[:, 3], red[:, 3]))
                    nc.vector.tensor_tensor(comb[:], ex[:], over_experts(3), ALU.mult).then_inc(s_comb, 1)
                    dve.wait_ge(s_comb, m + 1)

                def place_samples():
                    then = chain(s_place, 12, p)
                    dve.wait_ge(s_p_off, p + 1)
                    dve.wait_ge(s_p_tanh, count(p))
                    nc.vector.tensor_tensor(po[:], ps_m[:, 0:TILES * 32].rearrange(
                        "p (t k) -> p t k", k=32)[:, :, 0:OFF], offb[:], ALU.add).then_inc(s_p_po, 1)
                    dve.wait_ge(s_p_po, p + 1)

                    def tk(ap):
                        return ap.rearrange("p (t k) -> p t k", t=TILES)

                    nc.vector.scalar_tensor_tensor(tk(pos[:, 0]), tk(tapy[:]), rowbase[:, bass.ds(p, 1)],
                                                   po[:, :, 0:2 * TAPS:2], ALU.add, ALU.add)
                    then(nc.vector.tensor_tensor(tk(pos[:, 1]), tk(tapx[:]), po[:, :, 1:2 * TAPS:2], ALU.add))
                    then(nc.vector.tensor_scalar(pos[:], pos[:], -1.0, float(HW), ALU.max, ALU.min))
                    then(nc.vector.tensor_copy(cell_i[:], pos[:]))
                    then(nc.vector.tensor_copy(cell[:], cell_i[:]))
                    then(nc.vector.tensor_tensor(over[:], cell[:], pos[:], ALU.is_gt))
                    then(nc.vector.tensor_tensor(cell[:], cell[:], over[:], ALU.subtract))
                    then(nc.vector.tensor_scalar(cell[:], cell[:], float(HW - 1), None, ALU.min))
                    then(nc.vector.tensor_tensor(hi_w[:], pos[:], cell[:], ALU.subtract))
                    then(nc.vector.tensor_scalar(lo_w[:], hi_w[:], -1.0, 1.0, ALU.mult, ALU.add))
                    dve.wait_ge(s_p_tanh, p + 1)
                    then(nc.vector.tensor_scalar(mask[:], mask[:], 0.5, 0.5, ALU.mult, ALU.add))
                    nc.vector.tensor_tensor(my[:, 0], lo_w[:, 0], mask[:], ALU.mult)
                    then(nc.vector.tensor_tensor(my[:, 1], hi_w[:, 0], mask[:], ALU.mult))
                    then(nc.vector.scalar_tensor_tensor(flat[:], cell[:, 0], float(TW), cell[:, 1], ALU.mult, ALU.add))
                    for c in range(4):
                        nc.vector.tensor_tensor(w_ring[:, p % RING, c], my[:, c % 2],
                                                (lo_w if c < 2 else hi_w)[:, 1], ALU.mult)
                    nc.vector.tensor_scalar(idx_ring[:, p % RING], flat[:], idxbase[:, bass.ds(p, 1)], None,
                                            ALU.add).then_inc(s_p_done, 1)

                if on["B"]:
                    dve.wait_ge(s_p_done, g + 1)
                    dve.wait_ge(s_samp, count(SAMP * g))
                    nc.vector.tensor_copy(w_dve[:], w_ring[:, g % RING, 1:4]).then_inc(s_wdve, 1)
                    dve.wait_ge(s_wdve, g + 1)
                for j in range(PAIRS):
                    if on["B"]:
                        blend(j)
                    if j == 0 and on["M"]:
                        finish_tile(TILES - 1, m)
                    if j == 1 and on["M"]:
                        norm_tile(TILES - 1, m)
                    if j in (1, 2) and on["O"]:
                        add_expert(E - 3 + j, o)
                    if j == 3 and on["A"]:
                        channel_stats()
                    if j == 3 and on["M"]:
                        top2()
                    if j == 4 and on["A"]:
                        norm_channels()
                    if j == 5 and on["M"]:
                        dve.wait_ge(s_o_t, count(CC * m))
                        nc.vector.tensor_tensor(acc[:], x1[:], z[:], ALU.add).then_inc(s_acc0, 1)
                        dve.wait_ge(s_ct_t, m + 1)
                        nc.vector.tensor_copy(combT[:].rearrange("p t n -> p (t n)"), ps_y[1][0:E]).then_inc(s_ct, 1)
                        dve.wait_ge(s_acc0, m + 1)
                    if j == 6 and on["M"]:
                        for t in range(TILES):
                            dve.wait_ge(s_y, YUSES * m + t + 1)
                            nc.vector.tensor_tensor(acc[:, t], ps_y[t % 2][:, 0:C], acc[:, t],
                                                    ALU.add).then_inc(s_acc, 1)
                    if j >= 7 and j % 2 == 1 and on["M"]:
                        add_expert((j - 7) // 2, m)
                    if on["B"] and j - 2 in ends_at:
                        finish_tile(ends_at[j - 2], g)
                    if on["B"] and (j - 4 in ends_at or j == PAIRS - 1):
                        norm_tile(ends_at.get(j - 4, 2), g)
                    if j == 11 and on["P"]:
                        place_samples()

            iterate(dve, body)

        @block.tensor
        def _(pe):
            pe.wait_ge(s_ident, 16)

            def body(i, on):
                a, p, g, m, o = i, i - LAG_P, i - LAG_B, i - LAG_M, i - LAG_O

                if isinstance(i, int) and i == LAG_P:
                    pe.wait_ge(s_const, 16 * N_CONST)
                    pe.wait_ge(s_zero, 2)

                def transpose_pair(j):
                    pe.wait_ge(s_samp, SAMP * g + 2 * j + 2)
                    pe.wait_ge(s_sampT, count(PAIRS * g + j - 1))
                    for h in range(2):
                        for cc in range(CC):
                            ins = nc.tensor.transpose(ps_t[j % 2][:, h, cc],
                                                      samp[:, (2 * j + h) % SRING, cc * PT:(cc + 1) * PT], ident[:])
                    ins.then_inc(s_trans, 1)

                def convolve_pair(j):
                    pe.wait_ge(s_sampT, PAIRS * g + j + 1)
                    for h in range(2):
                        t, k = tile_of(2 * j + h)
                        dst = ps_conv[t % 2][:, 0:C]
                        if k == 0:
                            pe.wait_ge(s_x1, count(TILES * g + t - 1))
                            if t == 0:
                                pe.wait_ge(s_xb, 16 * g + 16)
                            for cc in range(CC):
                                ins = nc.tensor.matmul(dst[:, cc * PT:(cc + 1) * PT], xb[:, cc, t * PT:(t + 1) * PT],
                                                       ident[:], start=(cc == 0), stop=False, is_transpose=True,
                                                       skip_group_check=True)
                            if t == TILES - 1:
                                ins.then_inc(s_xb_used, 1)
                        for cc in range(CC):
                            ins = nc.tensor.matmul(dst, sampT[:, j % TRING, h, cc], convw[:, k, cc],
                                                   start=False, stop=(k == TAPS - 1 and cc == CC - 1),
                                                   skip_group_check=True)
                    ins.then_inc(s_conv, 1)

                def first_product(e, fc):
                    pe.wait_ge(s_g, count(CC * E * m + CC * e + fc))
                    pe.wait_ge(s_zt, CC * m + CC)
                    for cc in range(CC):
                        ins = nc.tensor.matmul(ps_h[:], w1s[:, e, cc, fc * PT:(fc + 1) * PT], zT[:, cc],
                                               start=(cc == 0), stop=(cc == CC - 1))
                    ins.then_inc(s_h, 1)

                def second_product(e, mm):
                    pe.wait_ge(s_g, CC * E * mm + CC * e + CC)
                    for t in range(TILES):
                        use = TILES * (e + 1) + t
                        pe.wait_ge(s_acc, count(YUSES * mm + use - 1))
                        for fc in range(CC):
                            ins = nc.tensor.matmul(ps_y[use % 2][:, 0:C], hT[:, e % 2, fc, t * PT:(t + 1) * PT],
                                                   w2s[:, e, fc], start=(fc == 0), stop=(fc == CC - 1))
                        ins.then_inc(s_y, 1)

                def misc_bank_free():
                    pe.wait_ge(s_p_po, count(min(p, groups) if isinstance(i, int) else (p if on["P"] else groups)))

                for j in range(PAIRS):
                    first_half = j >= 3 and j % 2 == 1 and on["M"]
                    if first_half:
                        first_product((j - 3) // 2, 0)
                    if on["B"]:
                        if j:
                            convolve_pair(j - 1)
                        transpose_pair(j)
                    if first_half:
                        first_product((j - 3) // 2, 1)
                    if j in (0, 1) and on["O"]:
                        second_product(E - 2 + j, o)
                    if j in (0, 2) and on["A"]:
                        q = j // 2
                        pe.wait_ge(s_xa, 16 * a + 16)
                        pe.wait_ge(s_a_rows, count(2 * a))
                        misc_bank_free()
                        pe.wait_ge(s_a_raw, count(2 * a + q))
                        if q and on["M"]:
                            pe.wait_ge(s_zt, CC * m + CC)
                        for t in (2 * q, 2 * q + 1):
                            for cc in range(CC):
                                col = (t % 2) * C + cc * PT
                                ins = nc.tensor.transpose(ps_m[:, col:col + PT],
                                                          xa[:, cc, t * PT:(t + 1) * PT], ident[:])
                        ins.then_inc(s_a_tok, 1)
                    if j == 1 and on["M"]:
                        pe.wait_ge(s_z, TILES * m + TILES)
                        pe.wait_ge(s_g, count(CC * E * m))
                        if on["A"]:
                            pe.wait_ge(s_a_raw, 2 * a + 1)
                        misc_bank_free()
                        pe.wait_ge(s_o, count(CC * (m - 1)))
                        for cc in range(CC):
                            for t in range(TILES):
                                ins = nc.tensor.transpose((ps_h, ps_m)[cc][:, t * PT:(t + 1) * PT],
                                                          z[:, t, cc * PT:(cc + 1) * PT], ident[:])
                            ins.then_inc(s_zt_t, 1)
                    if j == 2 and on["M"]:
                        pe.wait_ge(s_zt, CC * m + CC)
                        pe.wait_ge(s_acc, count(YUSES * m))
                        for t in range(TILES):
                            for cc in range(CC):
                                ins = nc.tensor.matmul(ps_y[0][:, t * E:(t + 1) * E], zT[:, cc, t * PT:(t + 1) * PT],
                                                       rw[:, cc], start=(cc == 0), stop=(cc == CC - 1))
                        ins.then_inc(s_logit, 1)
                    if j in (3, 4) and on["O"]:
                        cc = j - 3
                        pe.wait_ge(s_acc, YUSES * o + YUSES)
                        if on["A"]:
                            pe.wait_ge(s_a_raw, 2 * a + 2)
                        if on["M"]:
                            pe.wait_ge(s_zt, CC * m + CC)
                        misc_bank_free()
                        pe.wait_ge(s_o, count(CC * o + cc))
                        for t in range(TILES):
                            ins = nc.tensor.transpose(ps_m[:, t * PT:(t + 1) * PT],
                                                      acc[:, t, cc * PT:(cc + 1) * PT], ident[:])
                        ins.then_inc(s_o_t, 1)
                    if j == 4 and on["M"]:
                        pe.wait_ge(s_comb, m + 1)
                        for t in range(TILES):
                            ins = nc.tensor.transpose(ps_y[1][0:E, t * PT:(t + 1) * PT], comb[:, t], ident[:])
                        ins.then_inc(s_ct_t, 1)
                    if j == 5 and on["M"]:
                        pe.wait_ge(s_ct, m + 1)
                        for t in range(TILES):
                            if t >= 2:
                                pe.wait_ge(s_acc, count(YUSES * m + t - 1))
                            nc.tensor.matmul(ps_y[t % 2][:, 0:C], combT[:, t], b2s[:], start=True,
                                             stop=True).then_inc(s_y, 1)
                    if j in (5, 6) and on["A"]:
                        q = j - 5
                        pe.wait_ge(s_a_norm, a + 1)
                        if on["O"]:
                            pe.wait_ge(s_o, CC * o + CC)
                        pe.wait_ge(s_a_rows, count(2 * a + q))
                        for t in (2 * q, 2 * q + 1):
                            for cc in range(CC):
                                col = cc * 2 * PT + (t % 2) * PT
                                ins = nc.tensor.transpose(ps_m[:, col:col + PT],
                                                          xn[:, t, cc * PT:(cc + 1) * PT], ident[:])
                        ins.then_inc(s_a_back, 1)
                    if j >= 6 and j % 2 == 0 and on["M"]:
                        second_product((j - 6) // 2, m)
                    if j == 8 and on["P"]:
                        pe.wait_ge(s_a_rows, count(2 * a + 2 if on["A"] else 2 * groups))
                        if on["O"]:
                            pe.wait_ge(s_o, CC * o + CC)
                        misc_bank_free()
                        for n, (ky, cc) in enumerate((ky, cc) for ky in range(3) for cc in range(CC)):
                            row = (p % GPI) * ROWS + ky
                            src = chan[:, cc, bass.ds(row, ROWS), :].rearrange("p r w -> p (r w)")
                            ins = nc.tensor.matmul(ps_m[0:96], offw[:, cc, ky].rearrange("p x o -> p (x o)"), src,
                                                   start=(n == 0), stop=(n == 5))
                        ins.then_inc(s_p_conv, 1)
                    if j == 10 and on["P"]:
                        pe.wait_ge(s_p_shift, p + 1)
                        for t in range(TILES):
                            lhs = shifted[:, 2 * t:2 * t + 2, :].rearrange("p r w -> p (r w)")
                            ins = nc.tensor.matmul(ps_m[:, t * 32:t * 32 + OFF], lhs, stack[:],
                                                   start=True, stop=True)
                        ins.then_inc(s_p_off, 1)
                if on["B"]:
                    convolve_pair(PAIRS - 1)

            iterate(pe, body)


def run_inputs(np, x, L0_conv_weight, L0_conv_bias, L0_conv_p_weight, L0_conv_p_bias,
               L0_ffn_router_w, L0_ffn_w1, L0_ffn_b1, L0_ffn_w2, L0_ffn_b2):
    groups = x.shape[0] * GPI
    p = np.arange(PT)
    t, k = np.arange(SAMP) // TAPS, np.arange(SAMP) % TAPS
    g = np.arange(groups)
    f32 = np.float32
    every = np.ones((PT, 1), f32)
    arrays = {
        "xg": x.reshape(-1, CC, PT, GPI, GT).transpose(0, 3, 2, 1, 4).reshape(groups, PT, CC, GT),
        "conv_w": L0_conv_weight.reshape(C, CC, PT, TAPS).transpose(2, 3, 1, 0),
        "conv_b": L0_conv_bias,
        "off_w": L0_conv_p_weight.reshape(OFF, CC, PT, 3, 3).transpose(2, 1, 3, 4, 0),
        "off_b": L0_conv_p_bias.reshape(OFF),
        "router_w": L0_ffn_router_w.reshape(E, CC, PT).transpose(2, 1, 0),
        "w1": L0_ffn_w1.reshape(E, CC, PT, C).transpose(2, 0, 1, 3),
        "b1": L0_ffn_b1.reshape(E, CC, PT).transpose(2, 0, 1),
        "w2": L0_ffn_w2.reshape(E, CC, PT, C).transpose(2, 0, 1, 3),
        "b2": L0_ffn_b2,
        "ident_c": np.eye(PT, dtype=f32),
        "stack_c": np.vstack([np.eye(32, OFF, dtype=f32)] * 3),
        "tapy_c": every * (2 * t + k // 3).astype(f32),
        "tapx_c": (p[:, None] % HW + k % 3 - 1).astype(f32),
        "rowbase_c": ((g % GPI) * ROWS + p[:, None] // HW - 1).astype(f32),
        "idxbase_c": every * ((g // GPI) * (TH * TW) + TW + 1).astype(f32),
        "rev_c": np.ones((PT, TILES, 1), f32) * (E - np.arange(E)).astype(f32),
    }
    return groups, {n: np.ascontiguousarray(a) for n, a in arrays.items()}


def kernel(**inputs):
    import numpy as np
    import concourse.bacc as bacc
    from concourse.bass_utils import run_bass_kernel_spmd

    groups, arrays = run_inputs(np, **{n: np.asarray(a) for n, a in inputs.items()})
    nc = bacc.Bacc("TRN2", target_bir_lowering=False, num_devices=1)
    args = [nc.dram_tensor(n, a.shape, mybir.dt.from_np(a.dtype), kind="ExternalInput").ap()
            for n, a in arrays.items()]
    out = nc.dram_tensor("out", (groups, PT, CC, GT), F32, kind="ExternalOutput").ap()
    build(nc, groups, *args, out)
    r = run_bass_kernel_spmd(nc, [arrays], core_ids=[0]).results[0]["out"]
    return r.reshape(-1, GPI, PT, CC, GT).transpose(0, 3, 2, 1, 4).reshape(inputs["x"].shape)
```

```python
from contextlib import ExitStack

import concourse.bass as bass
from concourse import mybir

F32 = mybir.dt.float32
F32R = mybir.dt.float32r
I32 = mybir.dt.int32
ALU = mybir.AluOpType
ACT = mybir.ActivationFunctionType
AX = mybir.AxisListType.X

PT = 128
C = 256
CC = C // PT
HW = 64
TILES = 4
GT = TILES * PT
ROWS = GT // HW
GPI = HW // ROWS
TAPS = 9
OFF = 3 * TAPS
TW = HW + 2
TH = HW + 1
ENT = 2 * C
SAMP = TILES * TAPS
PAIRS = SAMP // 2
GRING = 6
SRING = 6
TRING = 2
E = 8
LN_C_EPS, LN_T_EPS = 1e-6, 1e-5
RING = 9
WCHUNK = 2 * C
STAGES = 2 * (GRING - 1)
CRING = 3
CROWS = ROWS + 2
FILLS = GPI - 2
LAG_P, LAG_B, LAG_M, LAG_O = 1, 9, 10, 11


def build(nc, groups, xg, conv_w, conv_b, off_w, off_b, router_w, w1, b1, w2, b2,
          ident_c, stack_c, tapy_c, tapx_c, rowbase_c, idxbase_c, inner_c, rev_c, out):
    images = groups // GPI
    table = nc.dram_tensor("patch_table", (images * TH * TW, ENT), F32, kind="Internal").ap()

    ctx = ExitStack()
    with ctx:
        def sb(name, shape, dt=F32):
            return ctx.enter_context(nc.sbuf_tensor(name, shape, dt))

        def bank(name, shape):
            return ctx.enter_context(nc.psum_tensor(name, shape, F32))

        def sem(name):
            return ctx.enter_context(nc.semaphore(name))

        convw = [sb(f"convw{n}", [PT, TAPS, CC, C], F32R) for n in ("_hi", "_lo")]
        convb = sb("convb", [PT, C])
        offw = sb("offw", [PT, CC, 3, 3, 32])
        offb = sb("offb", [PT, TILES, OFF])
        rw_raw = sb("rw_raw", [PT, CC, E])
        rw = [sb(f"rw{n}", [PT, CC, E], F32R) for n in ("_hi", "_lo")]
        w1s = [sb(f"w1{n}", [PT, E, CC, C], F32R) for n in ("_hi", "_lo")]
        w2s = sb("w2s", [PT, E, CC, C])
        b1s = sb("b1s", [PT, E, CC])
        b2s = sb("b2s", [E, C])
        ident = sb("ident", [PT, PT])
        stack = sb("stack", [96, OFF])
        tapy = sb("tapy", [PT, SAMP])
        tapx = sb("tapx", [PT, SAMP])
        rowbase = sb("rowbase", [PT, groups])
        idxbase = sb("idxbase", [PT, groups])
        rev = sb("rev", [PT, TILES, E])
        minus_half = sb("minus_half", [PT, TILES])
        inner = sb("inner", [PT, 2, groups])
        xa = sb("xa", [PT, CC, GT])
        xn = sb("xn", [PT, TILES, C])
        chan = sb("chan", [PT, CC, CRING, CROWS, HW])
        st_a = sb("st_a", [PT, TILES, 6])
        mv_a = sb("mv_a", [PT, TILES, 2])
        ve_a = sb("ve_a", [PT, TILES])
        rs_a = sb("rs_a", [PT, TILES])
        shifted = sb("shifted", [96, ROWS, HW])
        po = sb("po", [PT, TILES, OFF])
        pos = sb("pos", [PT, 2, SAMP])
        cell_i = sb("cell_i", [PT, 2, SAMP], I32)
        cell = sb("cell", [PT, 2, SAMP])
        over = sb("over", [PT, 2, SAMP])
        hi_w = sb("hi_w", [PT, 2, SAMP])
        lo_w = sb("lo_w", [PT, 2, SAMP])
        mask = sb("mask", [PT, SAMP])
        my = sb("my", [PT, 2, SAMP])
        flat = sb("flat", [PT, SAMP])
        idx_ring = sb("idx_ring", [PT, RING, SAMP], I32)
        w_ring = sb("w_ring", [PT, RING, 4, SAMP])
        idx = sb("idx", [PT, SAMP], I32)
        w_act = sb("w_act", [PT, SAMP])
        w_dve = sb("w_dve", [PT, 3, SAMP])
        patch = sb("patch", [PT, GRING, 4 * C])
        zeros = patch[:, 0, 0:ENT]
        stage = patch[:, 1:GRING].rearrange("p s (h n) -> p (s h) n", n=WCHUNK)
        samp = sb("samp", [PT, SRING, C])
        sampT = [sb(f"sampT{n}", [PT, TRING, 2, CC, PT], F32R) for n in ("_hi", "_lo")]
        xb = sb("xb", [PT, CC, GT])
        x1 = sb("x1", [PT, TILES, C])
        z = sb("z", [PT, TILES, C])
        st_b = sb("st_b", [PT, 6])
        mv_b = sb("mv_b", [PT, 2])
        ve_b = sb("ve_b", [PT, 1])
        rs_b = sb("rs_b", [PT, 1])
        zT = [sb(f"zT{n}", [PT, CC, GT], F32R) for n in ("_hi", "_lo")]
        lg = sb("lg", [PT, TILES, E])
        lg2 = sb("lg2", [PT, TILES, E])
        cand = sb("cand", [PT, TILES, E])
        hot1 = sb("hot1", [PT, TILES, E])
        hot2 = sb("hot2", [PT, TILES, E])
        ex = sb("ex", [PT, TILES, E])
        red = sb("red", [PT, 6, TILES])
        comb = sb("comb", [PT, TILES, E])
        combT = sb("combT", [E, TILES, PT])
        hT = sb("hT", [PT, 2, CC, GT])
        acc = sb("acc", [PT, TILES, C])
        outT = xa

        ps_t = [bank(f"ps_t{i}", [PT, 2, CC, PT]) for i in range(2)]
        ps_conv = [bank(f"ps_conv{i}", [PT, GT]) for i in range(2)]
        ps_m = bank("ps_m", [PT, GT])
        ps_h = bank("ps_h", [PT, GT])
        ps_y = [bank(f"ps_y{i}", [PT, GT]) for i in range(2)]

        s_ident = sem("s_ident")
        s_const = sem("s_const")
        s_zero = sem("s_zero")
        s_offw0 = sem("s_offw0")
        s_pad = sem("s_pad")
        s_xa = sem("s_xa")
        s_xb = sem("s_xb")
        s_tab = sem("s_tab")
        s_out = sem("s_out")
        s_patch = [sem(f"s_patch{i}") for i in range(GRING)]
        s_idx = sem("s_idx")
        s_a_tok = sem("s_a_tok")
        s_a_raw = sem("s_a_raw")
        s_a_norm = sem("s_a_norm")
        s_a_back = sem("s_a_back")
        s_a_rows = sem("s_a_rows")
        s_p_conv = sem("s_p_conv")
        s_p_shift = sem("s_p_shift")
        s_p_off = sem("s_p_off")
        s_p_po = sem("s_p_po")
        s_p_tanh = sem("s_p_tanh")
        s_p_done = sem("s_p_done")
        s_wact = sem("s_wact")
        s_first = sem("s_first")
        s_samp = sem("s_samp")
        s_trans = sem("s_trans")
        s_sampT = sem("s_sampT")
        s_low = sem("s_low")
        s_conv = sem("s_conv")
        s_x1 = sem("s_x1")
        s_z = sem("s_z")
        s_xb_used = sem("s_xb_used")
        s_zt_t = sem("s_zt_t")
        s_zt = sem("s_zt")
        s_zt_low = sem("s_zt_low")
        s_stage = [sem(f"s_stage{i}") for i in range(STAGES)]
        s_w_hi = sem("s_w_hi")
        s_w_lo = sem("s_w_lo")
        s_logit = sem("s_logit")
        s_lg = sem("s_lg")
        s_ex = sem("s_ex")
        s_comb = sem("s_comb")
        s_ct_t = sem("s_ct_t")
        s_ct = sem("s_ct")
        s_h = sem("s_h")
        s_g = sem("s_g")
        s_b2 = sem("s_b2")
        s_bias = sem("s_bias")
        s_y = sem("s_y")
        s_acc = sem("s_acc")
        s_o_t = sem("s_o_t")
        s_o = sem("s_o")
        s_var_a = sem("s_var_a")
        s_rstd_a = sem("s_rstd_a")
        s_var = sem("s_var")
        s_rstd = sem("s_rstd")
        s_ve = sem("s_ve")
        s_ve_a = sem("s_ve_a")
        s_wdve = sem("s_wdve")
        s_acc0 = sem("s_acc0")
        s_seen_dve = sem("s_seen_dve")
        s_seen_pool = sem("s_seen_pool")
        s_st_a = sem("s_st_a")
        s_place = sem("s_place")
        s_blend = sem("s_blend")
        s_fin = sem("s_fin")
        s_top = sem("s_top")
        YUSES = TILES * E

        def first_at(j):
            n = j - 3 if j >= 3 else j + PAIRS - 3
            return (n // CC, n % CC, j < 3) if n < CC * E else None

        def second_at(j):
            n = j - 5 if j >= 5 else j + PAIRS - 5
            return (n // 2, n % 2, j < 5) if n < 2 * E else None

        CHUNKS = [(conv_w[:, k], convw[0][:, k], convw[1][:, k]) for k in range(TAPS)]
        CHUNKS += [(w1[:, e], w1s[0][:, e], w1s[1][:, e]) for e in range(E)]
        CHUNKS = [tuple(ap.rearrange("p a n -> p (a n)") for ap in chunk) for chunk in CHUNKS]
        CONSTS = [(convb, conv_b.partition_broadcast(PT)), (rw_raw, router_w), (w2s, w2),
                  (b1s, b1), (b2s, b2), (stack, stack_c), (tapy, tapy_c), (tapx, tapx_c),
                  (rowbase, rowbase_c), (idxbase, idxbase_c), (rev, rev_c)]
        N_CONST = len(CONSTS) + CC * 3 + TILES
        N_PAD = 4 + (FILLS if images > 1 else 0)

        last = groups + LAG_O
        cuts = sorted({0, 1, 2, GPI, LAG_B, LAG_B + 1, LAG_B + 2, LAG_B + 3, groups, groups + 1, groups + LAG_B,
                       groups + LAG_B + 1, last})
        segments = [(a, b) for a, b in zip(cuts, cuts[1:])]

        def active(i):
            return {s: 0 <= i - lag < groups
                    for s, lag in (("A", 0), ("P", LAG_P), ("B", LAG_B), ("M", LAG_M), ("O", LAG_O))}

        assert (2, GPI) in segments

        def iterate(eng, body):
            for lo, hi in segments:
                if hi - lo == 1:
                    body(lo, active(lo))
                else:
                    with eng.Fori(lo, hi) as i:
                        body(i, active(lo))

        def count(value):
            return max(value, 0) if isinstance(value, int) else value

        def tile_of(s):
            return s // TAPS, s % TAPS

        ends_at = {(TAPS * t + TAPS - 1) // 2: t for t in range(TILES)}

        block = ctx.enter_context(nc.Block())

        @block.sync
        def _(sp):
            def load_chunk(n):
                sp.dma_start(stage[:, n % STAGES], CHUNKS[n][0]).then_inc(s_stage[n % STAGES], 16)

            def body(i, on):
                a = i
                a, o = i, i - LAG_O
                fills = on["P"] and not on["B"] and not isinstance(i, int)
                if isinstance(i, int) and i == GPI:
                    sp.wait_ge(s_pad, 16 * N_PAD)
                if on["A"]:
                    sp.wait_ge(s_a_tok, count(2 * a))
                    if on["O"]:
                        sp.wait_ge(s_out, 16 * o)
                    sp.dma_start(xa[:], xg[a]).then_inc(s_xa, 16)
                if isinstance(i, int) and i == 0:
                    sp.dma_start(ident[:], ident_c).then_inc(s_ident, 16)
                    sp.dma_start(inner[:], inner_c).then_inc(s_ident, 16)
                    for dst, src in CONSTS:
                        sp.dma_start(dst[:], src).then_inc(s_const, 16)
                    sp.wait_ge(s_offw0, 1)
                    for cc in range(CC):
                        for ky in range(3):
                            sp.dma_start(offw[:, cc, ky, :, 0:OFF], off_w[:, cc, ky]).then_inc(s_const, 16)
                    for t in range(TILES):
                        sp.dma_start(offb[:, t], off_b.partition_broadcast(PT)).then_inc(s_const, 16)
                    for n in range(STAGES):
                        load_chunk(n)
                if isinstance(i, int) and i == 1:
                    for n in range(STAGES, len(CHUNKS)):
                        sp.wait_ge(s_w_lo, n - STAGES + 1)
                        load_chunk(n)
                    sp.wait_ge(s_zero, 1)
                    first = table[0:TH * TW].rearrange("(y x) e -> y x e", x=TW)
                    sp.dma_start(first[0, 1:HW + 1, 0:C], zeros[0:HW, 0:C]).then_inc(s_pad, 16)
                    sp.dma_start(first[HW, 1:HW + 1, C:ENT], zeros[0:HW, 0:C]).then_inc(s_pad, 16)
                    sp.dma_start(first[:, 0, :], zeros[0:TH, :]).then_inc(s_pad, 16)
                    sp.dma_start(first[:, TW - 1, :], zeros[0:TH, :]).then_inc(s_pad, 16)
                if fills and images > 1:
                    piece = (images - 1) * TH * TW // FILLS
                    rows = table[bass.ds(TH * TW + piece * (i - 2), piece), :]
                    sp.dma_start(rows.rearrange("(x y) e -> x y e", x=TH),
                                 zeros[0:TH].unsqueeze(1).broadcast_to([TH, piece // TH, ENT])).then_inc(s_pad, 16)
                if on["A"]:
                    sp.wait_ge(s_a_norm, a + 1)
                    entries = table.rearrange("(y x) e -> y x e", x=TW)
                    for half in range(2):
                        for r in range(2):
                            y = a * ROWS + a // GPI + (r + 1 - half)
                            dst = entries[bass.ds(y, TILES, 2), 1:HW + 1, half * C:(half + 1) * C]
                            sp.dma_start(dst.rearrange("t x c -> x t c"),
                                         xn[HW * r:HW * r + HW]).then_inc(s_tab, 16)
                if on["O"]:
                    sp.wait_ge(s_o, CC * o + CC)
                    sp.dma_start(out[o], outT[:]).then_inc(s_out, 16)

            iterate(sp, body)
            sp.wait_ge(s_out, 16 * groups)
            sp.wait_ge(s_tab, 64 * groups)
            sp.wait_ge(s_pad, 16 * N_PAD)

        @block.gpsimd
        def _(pool):
            nc.gpsimd.memset(zeros, 0.0).then_inc(s_zero, 1)
            nc.gpsimd.memset(minus_half[:], -0.5)
            nc.gpsimd.memset(offw[:], 0.0).then_inc(s_offw0, 1)
            nc.gpsimd.memset(shifted[:], 0.0)
            nc.gpsimd.memset(chan[:], 0.0).then_inc(s_zero, 1)

            def body(i, on):
                a, g, m = i, i - LAG_B, i - LAG_M

                if isinstance(i, int) and i == LAG_B:
                    pool.wait_ge(s_w_lo, len(CHUNKS))

                def rsqrt_tile(t, gg):
                    pool.wait_ge(s_var, TILES * gg + t + 1)
                    pool.wait_ge(s_z, count(TILES * gg + t))
                    pool.sem_inc(s_seen_pool, 1)
                    nc.gpsimd.tensor_scalar(ve_b[:], mv_b[:, 1:2], LN_T_EPS, None, ALU.add).then_inc(s_ve, 1)
                    pool.wait_ge(s_ve, TILES * gg + t + 1)
                    nc.gpsimd.tensor_tensor(rs_b[:], ve_b[:], minus_half[:, 0:1], ALU.pow).then_inc(s_rstd, 1)

                def rsqrt_channels():
                    pool.wait_ge(s_var_a, a + 1)
                    pool.wait_ge(s_a_norm, count(a))
                    pool.sem_inc(s_seen_pool, 1)
                    nc.gpsimd.tensor_scalar(ve_a[:], mv_a[:, :, 1], LN_C_EPS, None, ALU.add).then_inc(s_ve_a, 1)
                    pool.wait_ge(s_ve_a, a + 1)
                    nc.gpsimd.tensor_tensor(rs_a[:], ve_a[:], minus_half[:], ALU.pow).then_inc(s_rstd_a, 1)

                if not on["B"]:
                    if on["M"]:
                        rsqrt_tile(TILES - 1, m)
                    if on["A"]:
                        rsqrt_channels()
                    return
                pool.wait_ge(s_p_done, g + 1)
                for slot in range(GRING):
                    pool.wait_ge(s_patch[slot], count(16 * (SAMP // GRING) * g))
                nc.gpsimd.tensor_copy(idx[:], idx_ring[:, g % RING]).then_inc(s_idx, 1)
                pool.wait_ge(s_idx, g + 1)
                pool.wait_ge(s_tab, count(64 * GPI * (g // GPI) + 64 * GPI))
                pool.wait_ge(s_xb_used, count(g))
                pool.dma_start(xb[:], xg[g]).then_inc(s_xb, 16)
                for s in range(SAMP):
                    pool.wait_ge(s_pad, 16 * N_PAD)
                    pool.wait_ge(s_samp, count(SAMP * g + s - GRING + 1))
                    pool.sem_inc(s_seen_pool, 1)
                    nc.gpsimd.indirect_dma_start(
                        patch[:, s % GRING], None, table,
                        bass.IndirectOffsetOnAxis(idx[:, s:s + 1], 0)).then_inc(s_patch[s % GRING], 16)
                    if s == 7 and on["M"]:
                        rsqrt_tile(TILES - 1, m)
                    if s == 13 and on["A"]:
                        rsqrt_channels()
                    if s in (19, 27, 35):
                        rsqrt_tile((19, 27, 35).index(s), g)

            iterate(pool, body)

        @block.scalar
        def _(act):
            act.wait_ge(s_zero, 2)
            act.wait_ge(s_ident, 32)

            def body(i, on):
                a, p, g, m, o = i, i - LAG_P, i - LAG_B, i - LAG_M, i - LAG_O

                if isinstance(i, int) and i == LAG_P:
                    act.wait_ge(s_const, 16 * N_CONST)
                    for n, (_, high, _) in enumerate(CHUNKS):
                        act.wait_ge(s_stage[n % STAGES], 16 * (n // STAGES) + 16)
                        nc.scalar.copy(high, stage[:, n % STAGES]).then_inc(s_w_hi, 1)
                    nc.scalar.copy(rw[0][:], rw_raw[:]).then_inc(s_w_hi, 1)

                def first_corner(j):
                    for s in (2 * j, 2 * j + 1):
                        act.wait_ge(s_patch[s % GRING], 16 * (SAMP // GRING) * g + 16 * (s // GRING) + 16)
                        act.wait_ge(s_trans, count(PAIRS * g + j - SRING // 2 + 1))
                        nc.scalar.activation(samp[:, s % SRING], patch[:, s % GRING, 0:C], ACT.Copy,
                                             scale=w_act[:, s:s + 1]).then_inc(s_first, 1)

                def keep_pair(j):
                    act.wait_ge(s_trans, PAIRS * g + j + 1)
                    act.wait_ge(s_conv, count(PAIRS * g + j - TRING + 1))
                    nc.scalar.copy(sampT[0][:, j % TRING], ps_t[j % 2][:]).then_inc(s_sampT, 1)

                def gelu(e, fc, mm):
                    act.wait_ge(s_h, count(CC * E * mm + CC * e + fc + 1))
                    act.wait_ge(s_y, count(YUSES * mm + TILES * (e - 1)))
                    nc.scalar.activation(hT[:, e % 2, fc], ps_h[:], ACT.Gelu,
                                         bias=b1s[:, e, fc:fc + 1]).then_inc(s_g, 1)

                if on["B"]:
                    act.wait_ge(s_p_done, g + 1)
                    act.wait_ge(s_first, count(SAMP * g))
                    nc.scalar.copy(w_act[:], w_ring[:, g % RING, 0]).then_inc(s_wact, 1)
                    act.wait_ge(s_wact, g + 1)
                    first_corner(0)
                for j in range(PAIRS):
                    if on["B"] and j + 1 < PAIRS:
                        first_corner(j + 1)
                    if on["B"]:
                        keep_pair(j)
                    if j == 4 and on["M"]:
                        act.wait_ge(s_lg, m + 1)
                        nc.scalar.activation(ex[:], ex[:], ACT.Exp).then_inc(s_ex, 1)
                    if j == 12 and on["P"]:
                        act.wait_ge(s_p_po, p + 1)
                        act.wait_ge(s_p_done, count(p))
                        nc.scalar.activation(mask[:].rearrange("p (t k) -> p t k", t=TILES), po[:, :, 2 * TAPS:OFF],
                                             ACT.Tanh, scale=0.5).then_inc(s_p_tanh, 1)
                    if first_at(j) and on["O" if first_at(j)[2] else "M"]:
                        e, fc, late = first_at(j)
                        gelu(e, fc, o if late else m)
                    if j in (0, 2) and on["A"]:
                        q = j // 2
                        act.wait_ge(s_a_tok, 2 * a + q + 1)
                        act.wait_ge(s_tab, count(64 * a))
                        act.wait_ge(s_a_back, count(2 * a))
                        nc.scalar.copy(xn[:, 2 * q:2 * q + 2].rearrange("p t c -> p (t c)"),
                                       ps_m[:]).then_inc(s_a_raw, 1)
                    if j == 1 and on["M"]:
                        for cc in range(CC):
                            act.wait_ge(s_zt_t, CC * m + cc + 1)
                            act.wait_ge(s_h, count(CC * E * m))
                            nc.scalar.copy(zT[0][:, cc], (ps_h, ps_m)[cc][:]).then_inc(s_zt, 1)
                    if j in (4, 5) and on["O"]:
                        cc = j - 4
                        act.wait_ge(s_out, count(16 * o))
                        if on["A"]:
                            act.wait_ge(s_a_tok, 2 * a + 2)
                        act.wait_ge(s_o_t, CC * o + cc + 1)
                        nc.scalar.copy(outT[:, cc], ps_m[:]).then_inc(s_o, 1)
                    if j in (6, 7) and on["A"]:
                        q = j - 6
                        act.wait_ge(s_a_back, 2 * a + q + 1)
                        act.wait_ge(s_p_conv, count(a - 1))
                        half = ps_m[:].rearrange("p (c r w) -> p c r w", c=CC, w=HW)
                        slot, row, edge = ((a - 1) % CRING, CROWS - 1, 0) if q == 0 else ((a + 1) % CRING, 0, 3)
                        nc.scalar.activation(chan[:, :, slot, row], half[:, :, edge], ACT.Copy,
                                             scale=inner[:, q, bass.ds(a, 1)])
                        nc.scalar.copy(chan[:, :, a % CRING, 1 + 4 * q:5 + 4 * q].rearrange("p c r w -> p c (r w)"),
                                       half.rearrange("p c r w -> p c (r w)")).then_inc(s_a_rows, 1)
                    if j == 6 and isinstance(i, int) and i == groups:
                        act.wait_ge(s_p_conv, groups - 1)
                        nc.scalar.mul(chan[:, :, (groups - 1) % CRING, CROWS - 1], convb[:, 0:CC * HW].rearrange(
                            "p (c w) -> p c w", c=CC), 0.0).then_inc(s_a_rows, 1)
                    if j == 9 and on["P"]:
                        act.wait_ge(s_p_conv, p + 1)
                        act.wait_ge(s_p_off, count(p))
                        ps = ps_m[:].rearrange("p (r w) -> p r w", w=HW)
                        nc.scalar.copy(shifted[0:32, :, 1:HW], ps[0:32, :, 0:HW - 1])
                        nc.scalar.copy(shifted[32:64, :, :], ps[32:64, :, :])
                        nc.scalar.copy(shifted[64:96, :, 0:HW - 1], ps[64:96, :, 1:HW]).then_inc(s_p_shift, 1)

            iterate(act, body)

        @block.vector
        def _(dve):

            def body(i, on):
                a, p, g, m, o = i, i - LAG_P, i - LAG_B, i - LAG_M, i - LAG_O
                if isinstance(i, int) and i == LAG_P:
                    dve.wait_ge(s_const, 16 * N_CONST)
                    for n, (_, high, low) in enumerate(CHUNKS):
                        dve.wait_ge(s_w_hi, n + 1)
                        nc.vector.tensor_tensor(low, stage[:, n % STAGES], high.bitcast(F32),
                                                ALU.subtract).then_inc(s_w_lo, 1)
                    dve.wait_ge(s_w_hi, len(CHUNKS) + 1)
                    nc.vector.tensor_tensor(rw[1][:], rw_raw[:], rw[0][:].bitcast(F32),
                                            ALU.subtract).then_inc(s_w_lo, 1)

                def chain(semaphore, per_group, group, done=0):
                    links = [done]

                    def link(ins):
                        links[0] += 1
                        assert links[0] <= per_group
                        ins.then_inc(semaphore, 1)
                        dve.wait_ge(semaphore, count(per_group * group + links[0]))
                    return link

                def blend(j):
                    pair = (2 * j, 2 * j + 1)
                    for c in range(1, 4):
                        for s in pair:
                            src = patch[:, s % GRING, c * C:(c + 1) * C]
                            if c == 1:
                                dve.wait_ge(s_patch[s % GRING], 16 * (SAMP // GRING) * g + 16 * (s // GRING) + 16)
                                dve.wait_ge(s_first, SAMP * g + s + 1)
                            else:
                                dve.wait_ge(s_blend, count(2 * SAMP * g + 4 * j + 2 * (c - 2) + (s % 2) + 1))
                            ins = nc.vector.scalar_tensor_tensor(
                                samp[:, s % SRING], src, w_dve[:, c - 1, s:s + 1], samp[:, s % SRING],
                                ALU.mult, ALU.add)
                            ins.then_inc(s_samp if c == 3 else s_blend, 1)

                def low_parts(j):
                    dve.wait_ge(s_sampT, count(PAIRS * g + j + 1))
                    dve.wait_ge(s_conv, count(PAIRS * g + j - TRING + 1))
                    nc.vector.tensor_tensor(sampT[1][:, j % TRING], ps_t[j % 2][:],
                                            sampT[0][:, j % TRING].bitcast(F32), ALU.subtract).then_inc(s_low, 1)

                def finish_tile(t, gg):
                    dve.wait_ge(s_conv, count(PAIRS * gg + (TAPS * t + TAPS - 1) // 2 + 1))
                    ins = nc.vector.tensor_tensor(x1[:, t], ps_conv[t % 2][:, 0:C], convb[:], ALU.add)
                    ins.then_inc(s_x1, 1)
                    dve.wait_ge(s_x1, TILES * gg + t + 1)
                    nc.vector.bn_stats(st_b[:], x1[:, t]).then_inc(s_fin, 1)
                    dve.wait_ge(s_fin, TILES * gg + t + 1)
                    dve.sem_inc(s_seen_dve, 1)
                    nc.vector.bn_aggr(mv_b[:], st_b[:]).then_inc(s_var, 1)

                def norm_tile(t, gg):
                    dve.wait_ge(s_var, TILES * gg + t + 1)
                    dve.wait_ge(s_rstd, TILES * gg + t + 1)
                    dve.wait_ge(s_zt_t, count(CC * gg))
                    nc.vector.tensor_scalar(z[:, t], x1[:, t], mv_b[:, 0:1], rs_b[:], ALU.subtract,
                                            ALU.mult).then_inc(s_z, 1)

                def add_expert(e, half, mm):
                    for t in (2 * half, 2 * half + 1):
                        use = TILES * e + t
                        dve.wait_ge(s_y, count(YUSES * mm + use + 1))
                        dve.wait_ge(s_acc, count(YUSES * mm + use - TILES + 1))
                        nc.vector.scalar_tensor_tensor(acc[:, t], ps_y[use % 2][:, 0:C], comb[:, t, e:e + 1], acc[:, t],
                                                       ALU.mult, ALU.add).then_inc(s_acc, 1)

                def add_bias(half, mm):
                    dve.wait_ge(s_b2, 2 * mm + half + 1)
                    dve.wait_ge(s_acc, YUSES * mm + TILES * (5 + half) + 2)
                    nc.vector.tensor_tensor(acc[:, 2 * half:2 * half + 2].rearrange("p t c -> p (t c)"), ps_m[:],
                                            acc[:, 2 * half:2 * half + 2].rearrange("p t c -> p (t c)"),
                                            ALU.add).then_inc(s_bias, 1)
                    dve.wait_ge(s_bias, 2 * mm + half + 1)

                def channel_stats():
                    dve.wait_ge(s_a_raw, 2 * a + 2)
                    for t in range(TILES):
                        ins = nc.vector.bn_stats(st_a[:, t], xn[:, t])
                    ins.then_inc(s_st_a, 1)
                    dve.wait_ge(s_st_a, a + 1)
                    dve.sem_inc(s_seen_dve, 1)
                    for t in range(TILES):
                        ins = nc.vector.bn_aggr(mv_a[:, t], st_a[:, t])
                    ins.then_inc(s_var_a, 1)

                def norm_channels():
                    dve.wait_ge(s_var_a, a + 1)
                    dve.wait_ge(s_rstd_a, a + 1)
                    for t in range(TILES):
                        ins = nc.vector.tensor_scalar(xn[:, t], xn[:, t], mv_a[:, t, 0:1], rs_a[:, t:t + 1],
                                                      ALU.subtract, ALU.mult)
                    ins.then_inc(s_a_norm, 1)

                def over_experts(r):
                    return red[:, r].unsqueeze(2).broadcast_to([PT, TILES, E])

                def top2():
                    then = chain(s_top, 20, m)
                    dve.wait_ge(s_logit, m + 1)
                    dve.wait_ge(s_acc, count(YUSES * m))
                    then(nc.vector.tensor_copy(lg[:], ps_m[:, 0:TILES * E].rearrange("p (t e) -> p t e", e=E)))

                    then(nc.vector.tensor_reduce(red[:, 0], lg[:], AX, ALU.max))
                    nc.vector.tensor_tensor(ex[:], lg[:], over_experts(0), ALU.subtract).then_inc(s_lg, 1)
                    then(nc.vector.tensor_tensor(cand[:], lg[:], over_experts(0), ALU.is_equal))
                    then(nc.vector.tensor_tensor(cand[:], cand[:], rev[:], ALU.mult))
                    then(nc.vector.tensor_reduce(red[:, 1], cand[:], AX, ALU.max))
                    then(nc.vector.tensor_tensor(hot1[:], cand[:], over_experts(1), ALU.is_equal))
                    then(nc.vector.scalar_tensor_tensor(lg2[:], hot1[:], -3.0e38, lg[:], ALU.mult, ALU.add))
                    then(nc.vector.tensor_reduce(red[:, 1], lg2[:], AX, ALU.max))
                    then(nc.vector.tensor_tensor(cand[:], lg2[:], over_experts(1), ALU.is_equal))
                    then(nc.vector.tensor_tensor(cand[:], cand[:], rev[:], ALU.mult))
                    then(nc.vector.tensor_reduce(red[:, 1], cand[:], AX, ALU.max))
                    then(nc.vector.tensor_tensor(hot2[:], cand[:], over_experts(1), ALU.is_equal))
                    then(nc.vector.tensor_tensor(hot1[:], hot1[:], hot2[:], ALU.add))

                def combine_weights():
                    then = chain(s_top, 20, m, 13)
                    dve.wait_ge(s_ex, m + 1)
                    then(nc.vector.tensor_reduce(red[:, 2], ex[:], AX, ALU.add))
                    then(nc.vector.reciprocal(red[:, 2], red[:, 2]))
                    then(nc.vector.tensor_tensor(ex[:], ex[:], over_experts(2), ALU.mult))
                    then(nc.vector.tensor_tensor(ex[:], ex[:], hot1[:], ALU.mult))
                    then(nc.vector.tensor_reduce(red[:, 3], ex[:], AX, ALU.add))
                    then(nc.vector.tensor_scalar(red[:, 3], red[:, 3], 1e-12, None, ALU.max))
                    then(nc.vector.reciprocal(red[:, 3], red[:, 3]))
                    nc.vector.tensor_tensor(comb[:], ex[:], over_experts(3), ALU.mult).then_inc(s_comb, 1)
                    dve.wait_ge(s_comb, m + 1)

                def place_samples():
                    then = chain(s_place, 12, p)
                    dve.wait_ge(s_p_off, p + 1)
                    dve.wait_ge(s_p_tanh, count(p))
                    nc.vector.tensor_tensor(po[:], ps_m[:, 0:TILES * 32].rearrange(
                        "p (t k) -> p t k", k=32)[:, :, 0:OFF], offb[:], ALU.add).then_inc(s_p_po, 1)
                    dve.wait_ge(s_p_po, p + 1)

                    def tk(ap):
                        return ap.rearrange("p (t k) -> p t k", t=TILES)

                    nc.vector.scalar_tensor_tensor(tk(pos[:, 0]), tk(tapy[:]), rowbase[:, bass.ds(p, 1)],
                                                   po[:, :, 0:2 * TAPS:2], ALU.add, ALU.add)
                    then(nc.vector.tensor_tensor(tk(pos[:, 1]), tk(tapx[:]), po[:, :, 1:2 * TAPS:2], ALU.add))
                    then(nc.vector.tensor_scalar(pos[:], pos[:], -1.0, float(HW), ALU.max, ALU.min))
                    then(nc.vector.tensor_copy(cell_i[:], pos[:]))
                    then(nc.vector.tensor_copy(cell[:], cell_i[:]))
                    then(nc.vector.tensor_tensor(over[:], cell[:], pos[:], ALU.is_gt))
                    then(nc.vector.tensor_tensor(cell[:], cell[:], over[:], ALU.subtract))
                    then(nc.vector.tensor_scalar(cell[:], cell[:], float(HW - 1), None, ALU.min))
                    then(nc.vector.tensor_tensor(hi_w[:], pos[:], cell[:], ALU.subtract))
                    then(nc.vector.tensor_scalar(lo_w[:], hi_w[:], -1.0, 1.0, ALU.mult, ALU.add))

                def place_weights():
                    then = chain(s_place, 12, p, 9)
                    dve.wait_ge(s_p_tanh, p + 1)
                    then(nc.vector.tensor_scalar(mask[:], mask[:], 0.5, 0.5, ALU.mult, ALU.add))
                    nc.vector.tensor_tensor(my[:, 0], lo_w[:, 0], mask[:], ALU.mult)
                    then(nc.vector.tensor_tensor(my[:, 1], hi_w[:, 0], mask[:], ALU.mult))
                    then(nc.vector.scalar_tensor_tensor(flat[:], cell[:, 0], float(TW), cell[:, 1], ALU.mult, ALU.add))
                    for c in range(4):
                        nc.vector.tensor_tensor(w_ring[:, p % RING, c], my[:, c % 2],
                                                (lo_w if c < 2 else hi_w)[:, 1], ALU.mult)
                    nc.vector.tensor_scalar(idx_ring[:, p % RING], flat[:], idxbase[:, bass.ds(p, 1)], None,
                                            ALU.add).then_inc(s_p_done, 1)

                if on["B"]:
                    dve.wait_ge(s_p_done, g + 1)
                    dve.wait_ge(s_samp, count(SAMP * g))
                    nc.vector.tensor_copy(w_dve[:], w_ring[:, g % RING, 1:4]).then_inc(s_wdve, 1)
                    dve.wait_ge(s_wdve, g + 1)
                for j in range(PAIRS):
                    if on["B"]:
                        blend(j)
                        if j:
                            low_parts(j - 1)
                    if j == 0 and on["O"]:
                        add_expert(*second_at(PAIRS - 1)[:2], o)
                        add_bias(1, o)
                    if j == 0 and on["M"]:
                        finish_tile(TILES - 1, m)
                    if j == 1 and on["M"]:
                        norm_tile(TILES - 1, m)
                    if j and second_at(j - 1) and on["O" if second_at(j - 1)[2] else "M"] and j - 1 < 5:
                        e, half, late = second_at(j - 1)
                        add_expert(e, half, o if late else m)
                    if j == 2 and on["M"]:
                        for cc in range(CC):
                            dve.wait_ge(s_zt, CC * m + cc + 1)
                            dve.wait_ge(s_h, count(CC * E * m))
                            nc.vector.tensor_tensor(zT[1][:, cc], (ps_h, ps_m)[cc][:], zT[0][:, cc].bitcast(F32),
                                                    ALU.subtract).then_inc(s_zt_low, 1)
                    if j == 3 and on["A"]:
                        channel_stats()
                    if j == 4 and on["M"]:
                        top2()
                    if j == 4 and on["A"]:
                        norm_channels()
                    if j == 5 and on["M"]:
                        combine_weights()
                    if j == 6 and on["M"]:
                        dve.wait_ge(s_o_t, count(CC * m))
                        dve.wait_ge(s_z, TILES * m + TILES)
                        nc.vector.tensor_tensor(acc[:], x1[:], z[:], ALU.add).then_inc(s_acc0, 1)
                        dve.wait_ge(s_acc0, m + 1)
                    if j - 1 >= 5 and on["M"]:
                        e, half, _ = second_at(j - 1)
                        add_expert(e, half, m)
                    if j == 14 and on["M"]:
                        dve.wait_ge(s_ct_t, m + 1)
                        nc.vector.tensor_copy(combT[:].rearrange("p t n -> p (t n)"), ps_m[0:E]).then_inc(s_ct, 1)
                    if j == 16 and on["M"]:
                        add_bias(0, m)
                    if on["B"] and j - 2 in ends_at:
                        finish_tile(ends_at[j - 2], g)
                    if on["B"] and (j - 4 in ends_at or j == PAIRS - 1):
                        norm_tile(ends_at.get(j - 4, 2), g)
                    if j == 12 and on["P"]:
                        place_samples()
                    if j == 13 and on["P"]:
                        place_weights()
                if on["B"]:
                    low_parts(PAIRS - 1)

            iterate(dve, body)

        @block.tensor
        def _(pe):
            pe.wait_ge(s_ident, 32)
            PARTS = ((0, 0), (0, 1), (1, 0))

            def body(i, on):
                a, p, g, m, o = i, i - LAG_P, i - LAG_B, i - LAG_M, i - LAG_O

                if isinstance(i, int) and i == LAG_P:
                    pe.wait_ge(s_const, 16 * N_CONST)
                    pe.wait_ge(s_zero, 2)
                    pe.wait_ge(s_w_lo, len(CHUNKS) + 1)

                def transpose_pair(j):
                    pe.wait_ge(s_samp, SAMP * g + 2 * j + 2)
                    pe.wait_ge(s_low, count(PAIRS * g + j - 1))
                    for h in range(2):
                        for cc in range(CC):
                            ins = nc.tensor.transpose(ps_t[j % 2][:, h, cc],
                                                      samp[:, (2 * j + h) % SRING, cc * PT:(cc + 1) * PT], ident[:])
                    ins.then_inc(s_trans, 1)

                def convolve_pair(j):
                    pe.wait_ge(s_low, PAIRS * g + j + 1)
                    for h in range(2):
                        t, k = tile_of(2 * j + h)
                        dst = ps_conv[t % 2][:, 0:C]
                        if k == 0:
                            pe.wait_ge(s_x1, count(TILES * g + t - 1))
                            if t == 0:
                                pe.wait_ge(s_xb, 16 * g + 16)
                            for cc in range(CC):
                                ins = nc.tensor.matmul(dst[:, cc * PT:(cc + 1) * PT], xb[:, cc, t * PT:(t + 1) * PT],
                                                       ident[:], start=(cc == 0), stop=False, is_transpose=True,
                                                       skip_group_check=True)
                            if t == TILES - 1:
                                ins.then_inc(s_xb_used, 1)
                        for cc in range(CC):
                            for n, (x, w) in enumerate(PARTS):
                                ins = nc.tensor.matmul(dst, sampT[x][:, j % TRING, h, cc], convw[w][:, k, cc],
                                                       start=False, stop=(k == TAPS - 1 and cc == CC - 1 and n == 2),
                                                       skip_group_check=True)
                    ins.then_inc(s_conv, 1)

                def first_product(e, fc, mm):
                    pe.wait_ge(s_g, count(CC * E * mm + CC * e + fc))
                    pe.wait_ge(s_zt_low, CC * mm + CC)
                    for cc in range(CC):
                        for n, (x, w) in enumerate(PARTS):
                            ins = nc.tensor.matmul(ps_h[:], w1s[w][:, e, cc, fc * PT:(fc + 1) * PT], zT[x][:, cc],
                                                   start=(cc == 0 and n == 0), stop=(cc == CC - 1 and n == 2))
                    ins.then_inc(s_h, 1)

                def second_product(e, half, mm):
                    pe.wait_ge(s_g, CC * E * mm + CC * e + CC)
                    for t in (2 * half, 2 * half + 1):
                        use = TILES * e + t
                        pe.wait_ge(s_acc, count(YUSES * mm + use - 1))
                        for fc in range(CC):
                            ins = nc.tensor.matmul(ps_y[use % 2][:, 0:C], hT[:, e % 2, fc, t * PT:(t + 1) * PT],
                                                   w2s[:, e, fc], start=(fc == 0), stop=(fc == CC - 1))
                        ins.then_inc(s_y, 1)

                def misc_bank_free():
                    if on["O"]:
                        pe.wait_ge(s_bias, 2 * m)
                    pe.wait_ge(s_p_po, p if on["P"] else min(groups, count(p)) if isinstance(i, int) else groups)

                for j in range(PAIRS):
                    if on["B"]:
                        if j:
                            convolve_pair(j - 1)
                        transpose_pair(j)
                    if j in (4, 5) and on["O"]:
                        cc = j - 4
                        pe.wait_ge(s_acc, YUSES * o + YUSES)
                        if on["A"]:
                            pe.wait_ge(s_a_raw, 2 * a + 2)
                        if on["M"]:
                            pe.wait_ge(s_lg, m + 1)
                        misc_bank_free()
                        pe.wait_ge(s_o, count(CC * o + cc))
                        for t in range(TILES):
                            ins = nc.tensor.transpose(ps_m[:, t * PT:(t + 1) * PT],
                                                      acc[:, t, cc * PT:(cc + 1) * PT], ident[:])
                        ins.then_inc(s_o_t, 1)
                    if first_at(j) and on["O" if first_at(j)[2] else "M"]:
                        e, fc, late = first_at(j)
                        first_product(e, fc, o if late else m)
                    if second_at(j) and on["O" if second_at(j)[2] else "M"]:
                        e, half, late = second_at(j)
                        second_product(e, half, o if late else m)
                    if j in (0, 2) and on["A"]:
                        q = j // 2
                        pe.wait_ge(s_xa, 16 * a + 16)
                        pe.wait_ge(s_a_rows, count(2 * a))
                        misc_bank_free()
                        pe.wait_ge(s_a_raw, count(2 * a + q))
                        if q and on["M"]:
                            pe.wait_ge(s_zt_low, CC * m + CC)
                        for t in (2 * q, 2 * q + 1):
                            for cc in range(CC):
                                col = (t % 2) * C + cc * PT
                                ins = nc.tensor.transpose(ps_m[:, col:col + PT],
                                                          xa[:, cc, t * PT:(t + 1) * PT], ident[:])
                        ins.then_inc(s_a_tok, 1)
                    if j == 1 and on["M"]:
                        pe.wait_ge(s_z, TILES * m + TILES)
                        pe.wait_ge(s_g, count(CC * E * m))
                        if on["A"]:
                            pe.wait_ge(s_a_raw, 2 * a + 1)
                        misc_bank_free()
                        pe.wait_ge(s_o, count(CC * (m - 1)))
                        for cc in range(CC):
                            for t in range(TILES):
                                ins = nc.tensor.transpose((ps_h, ps_m)[cc][:, t * PT:(t + 1) * PT],
                                                          z[:, t, cc * PT:(cc + 1) * PT], ident[:])
                            ins.then_inc(s_zt_t, 1)
                    if j == 3 and on["M"]:
                        pe.wait_ge(s_zt_low, CC * m + CC)
                        if on["A"]:
                            pe.wait_ge(s_a_raw, 2 * a + 2)
                        for t in range(TILES):
                            for cc in range(CC):
                                for n, (x, w) in enumerate(PARTS):
                                    ins = nc.tensor.matmul(ps_m[:, t * E:(t + 1) * E],
                                                           zT[x][:, cc, t * PT:(t + 1) * PT], rw[w][:, cc],
                                                           start=(cc == 0 and n == 0), stop=(cc == CC - 1 and n == 2))
                        ins.then_inc(s_logit, 1)
                    if j == 13 and on["M"]:
                        pe.wait_ge(s_comb, m + 1)
                        if on["P"]:
                            pe.wait_ge(s_p_po, p + 1)
                        if on["O"]:
                            pe.wait_ge(s_o, CC * o + CC)
                        for t in range(TILES):
                            ins = nc.tensor.transpose(ps_m[0:E, t * PT:(t + 1) * PT], comb[:, t], ident[:])
                        ins.then_inc(s_ct_t, 1)
                    if j in (15, 17) and on["M"]:
                        half = (j - 15) // 2
                        pe.wait_ge(s_ct, m + 1)
                        pe.wait_ge(s_bias, count(2 * m + half))
                        for t in (2 * half, 2 * half + 1):
                            ins = nc.tensor.matmul(ps_m[:, (t % 2) * C:(t % 2 + 1) * C], combT[:, t], b2s[:],
                                                   start=True, stop=True)
                        ins.then_inc(s_b2, 1)
                    if j in (6, 7) and on["A"]:
                        q = j - 6
                        pe.wait_ge(s_a_norm, a + 1)
                        if on["O"]:
                            pe.wait_ge(s_o, CC * o + CC)
                        pe.wait_ge(s_a_rows, count(2 * a + q))
                        for t in (2 * q, 2 * q + 1):
                            for cc in range(CC):
                                col = cc * 2 * PT + (t % 2) * PT
                                ins = nc.tensor.transpose(ps_m[:, col:col + PT],
                                                          xn[:, t, cc * PT:(cc + 1) * PT], ident[:])
                        ins.then_inc(s_a_back, 1)
                    if j == 9 and on["P"]:
                        pe.wait_ge(s_a_rows, 2 * a + 2 if on["A"] else 2 * groups + 1)
                        if on["O"]:
                            pe.wait_ge(s_o, CC * o + CC)
                        misc_bank_free()
                        for n, (ky, cc) in enumerate((ky, cc) for ky in range(3) for cc in range(CC)):
                            src = chan[:, cc, p % CRING, ky:ky + ROWS].rearrange("p r w -> p (r w)")
                            ins = nc.tensor.matmul(ps_m[0:96], offw[:, cc, ky].rearrange("p x o -> p (x o)"), src,
                                                   start=(n == 0), stop=(n == 5))
                        ins.then_inc(s_p_conv, 1)
                    if j == 11 and on["P"]:
                        pe.wait_ge(s_p_shift, p + 1)
                        for t in range(TILES):
                            lhs = shifted[:, 2 * t:2 * t + 2, :].rearrange("p r w -> p (r w)")
                            ins = nc.tensor.matmul(ps_m[:, t * 32:t * 32 + OFF], lhs, stack[:],
                                                   start=True, stop=True)
                        ins.then_inc(s_p_off, 1)
                if on["B"]:
                    convolve_pair(PAIRS - 1)

            iterate(pe, body)


def run_inputs(np, x, L0_conv_weight, L0_conv_bias, L0_conv_p_weight, L0_conv_p_bias,
               L0_ffn_router_w, L0_ffn_w1, L0_ffn_b1, L0_ffn_w2, L0_ffn_b2):
    groups = x.shape[0] * GPI
    p = np.arange(PT)
    t, k = np.arange(SAMP) // TAPS, np.arange(SAMP) % TAPS
    g = np.arange(groups)
    f32 = np.float32
    every = np.ones((PT, 1), f32)
    arrays = {
        "xg": x.reshape(-1, CC, PT, GPI, GT).transpose(0, 3, 2, 1, 4).reshape(groups, PT, CC, GT),
        "conv_w": L0_conv_weight.reshape(C, CC, PT, TAPS).transpose(2, 3, 1, 0),
        "conv_b": L0_conv_bias,
        "off_w": L0_conv_p_weight.reshape(OFF, CC, PT, 3, 3).transpose(2, 1, 3, 4, 0),
        "off_b": L0_conv_p_bias.reshape(OFF),
        "router_w": L0_ffn_router_w.reshape(E, CC, PT).transpose(2, 1, 0),
        "w1": L0_ffn_w1.reshape(E, CC, PT, C).transpose(2, 0, 1, 3),
        "b1": L0_ffn_b1.reshape(E, CC, PT).transpose(2, 0, 1),
        "w2": L0_ffn_w2.reshape(E, CC, PT, C).transpose(2, 0, 1, 3),
        "b2": L0_ffn_b2,
        "ident_c": np.eye(PT, dtype=f32),
        "stack_c": np.vstack([np.eye(32, OFF, dtype=f32)] * 3),
        "tapy_c": every * (2 * t + k // 3).astype(f32),
        "tapx_c": (p[:, None] % HW + k % 3 - 1).astype(f32),
        "rowbase_c": ((g % GPI) * ROWS + p[:, None] // HW - 1).astype(f32),
        "idxbase_c": every * ((g // GPI) * (TH * TW) + TW + 1).astype(f32),
        "inner_c": (every[:, :, None] * np.stack([g % GPI != 0, g % GPI != GPI - 1])).astype(f32),
        "rev_c": np.ones((PT, TILES, 1), f32) * (E - np.arange(E)).astype(f32),
    }
    return groups, {n: np.ascontiguousarray(a) for n, a in arrays.items()}


def kernel(**inputs):
    import numpy as np
    import concourse.bacc as bacc
    from concourse.bass_utils import run_bass_kernel_spmd

    groups, arrays = run_inputs(np, **{n: np.asarray(a) for n, a in inputs.items()})
    nc = bacc.Bacc("TRN2", target_bir_lowering=False, num_devices=1)
    args = [nc.dram_tensor(n, a.shape, mybir.dt.from_np(a.dtype), kind="ExternalInput").ap()
            for n, a in arrays.items()]
    out = nc.dram_tensor("out", (groups, PT, CC, GT), F32, kind="ExternalOutput").ap()
    build(nc, groups, *args, out)
    r = run_bass_kernel_spmd(nc, [arrays], core_ids=[0]).results[0]["out"]
    return r.reshape(-1, GPI, PT, CC, GT).transpose(0, 3, 2, 1, 4).reshape(inputs["x"].shape)
```

```python
from contextlib import ExitStack

import concourse.bass as bass
from concourse import mybir

F32 = mybir.dt.float32
F32R = mybir.dt.float32r
I32 = mybir.dt.int32
ALU = mybir.AluOpType
ACT = mybir.ActivationFunctionType
AX = mybir.AxisListType.X

PT = 128
C = 256
CC = C // PT
HW = 64
TILES = 4
GT = TILES * PT
ROWS = GT // HW
GPI = HW // ROWS
TAPS = 9
OFF = 3 * TAPS
TW = HW + 2
TH = HW + 1
ENT = 2 * C
SAMP = TILES * TAPS
PAIRS = SAMP // 2
GRING = 6
SRING = 6
TRING = 2
E = 8
LN_C_EPS, LN_T_EPS = 1e-6, 1e-5
RING = 7
WCHUNK = 2 * C
STAGES = 2 * (GRING - 1)
CRING = 3
CROWS = ROWS + 2
FILLS = 6
LAG_T, LAG_P, LAG_X, LAG_B, LAG_M, LAG_O = 1, 2, 7, 8, 9, 10
COPIES = 2 * 32 + E
TABLES = 2


def build(nc, groups, xg, conv_w, conv_b, off_w, off_b, router_w, w1, b1, w2, b2,
          ident_c, tapy_c, tapx_c, rowbase_c, idxbase_c, inner_c, rev_c, out):
    images = groups // GPI
    table = nc.dram_tensor("patch_table", (min(images, TABLES) * TH * TW, ENT), F32, kind="Internal").ap()

    ctx = ExitStack()
    with ctx:
        def sb(name, shape, dt=F32):
            return ctx.enter_context(nc.sbuf_tensor(name, shape, dt))

        def bank(name, shape):
            return ctx.enter_context(nc.psum_tensor(name, shape, F32))

        def sem(name):
            return ctx.enter_context(nc.semaphore(name))

        convw = [sb(f"convw{n}", [PT, TAPS, CC, C], F32R) for n in ("_hi", "_lo")]
        convb = sb("convb", [PT, C])
        offw = sb("offw", [PT, CC, 3, 3, 32])
        offb = sb("offb", [PT, TILES, OFF])
        rw_raw = sb("rw_raw", [PT, CC, E])
        rw = sb("rw", [PT, CC, 2 * E], F32R)
        w1s = [sb(f"w1{n}", [PT, E, CC, C], F32R) for n in ("_hi", "_lo")]
        w2s = sb("w2s", [PT, E, CC, C])
        b1s = sb("b1s", [PT, E, CC])
        b2s = sb("b2s", [COPIES, C], F32R)
        ident = sb("ident", [PT, PT])
        tapy = sb("tapy", [PT, SAMP])
        tapx = sb("tapx", [PT, SAMP])
        rowbase = sb("rowbase", [PT, groups])
        idxbase = sb("idxbase", [PT, groups])
        rev = sb("rev", [PT, TILES, E])
        minus_half = sb("minus_half", [PT, TILES])
        inner = sb("inner", [PT, 2, groups])
        xa = sb("xa", [PT, CC, GT])
        xt = sb("xt", [PT, TILES, C])
        xn = sb("xn", [PT, TILES, C])
        chan = sb("chan", [PT, CC, CRING, CROWS, HW])
        st_a = sb("st_a", [PT, TILES, 6])
        mv_a = sb("mv_a", [PT, TILES, 2])
        ve_a = sb("ve_a", [PT, TILES])
        rs_a = sb("rs_a", [PT, TILES])
        shifted = sb("shifted", [96, ROWS, HW])
        po = sb("po", [PT, TILES, OFF])
        pos = sb("pos", [PT, 2, SAMP])
        cell_i = sb("cell_i", [PT, 2, SAMP], I32)
        cell = sb("cell", [PT, 2, SAMP])
        over = sb("over", [PT, 2, SAMP])
        hi_w = sb("hi_w", [PT, 2, SAMP])
        lo_w = sb("lo_w", [PT, 2, SAMP])
        mask = sb("mask", [PT, SAMP])
        my = sb("my", [PT, 2, SAMP])
        flat = sb("flat", [PT, SAMP])
        idx_ring = sb("idx_ring", [PT, RING, SAMP], I32)
        w_ring = sb("w_ring", [PT, RING, 4, SAMP])
        idx = [sb(f"idx{half}", [PT, PAIRS], I32) for half in range(2)]
        w_act = sb("w_act", [PT, SAMP])
        w_dve = sb("w_dve", [PT, 3, SAMP])
        patch = sb("patch", [PT, GRING, 4 * C])
        zeros = patch[:, 0, 0:ENT]
        stage = patch[:, 1:GRING].rearrange("p s (h n) -> p (s h) n", n=WCHUNK)
        samp = sb("samp", [PT, SRING, C])
        sampT = [sb(f"sampT{n}", [PT, TRING, 2, CC, PT], F32R) for n in ("_hi", "_lo")]
        xb = sb("xb", [PT, CC, GT])
        x1 = sb("x1", [PT, TILES, C])
        z = sb("z", [PT, TILES, C])
        b2_raw = z[0:COPIES, 0]
        st_b = sb("st_b", [PT, 6])
        mv_b = sb("mv_b", [PT, 2])
        ve_b = sb("ve_b", [PT, 1])
        rs_b = sb("rs_b", [PT, 1])
        zT = [sb(f"zT{n}", [PT, CC, GT], F32R) for n in ("_hi", "_lo")]
        lg = sb("lg", [PT, TILES, E])
        lg2 = sb("lg2", [PT, TILES, E])
        cand = sb("cand", [PT, TILES, E])
        hot1 = sb("hot1", [PT, TILES, E])
        hot2 = sb("hot2", [PT, TILES, E])
        ex = sb("ex", [PT, TILES, E])
        red = sb("red", [PT, 6, TILES])
        comb = sb("comb", [PT, TILES, COPIES])
        combT = sb("combT", [COPIES, TILES, PT], F32R)
        hT = sb("hT", [PT, 2, CC, GT])
        acc = sb("acc", [PT, TILES, C])
        outT = xa

        ps_t = [bank(f"ps_t{i}", [PT, 2, CC, PT]) for i in range(2)]
        ps_conv = [bank(f"ps_conv{i}", [PT, GT]) for i in range(2)]
        ps_m = bank("ps_m", [PT, GT])
        ps_h = bank("ps_h", [PT, GT])
        ps_y = [bank(f"ps_y{i}", [PT, GT]) for i in range(2)]

        s_ident = sem("s_ident")
        s_const = sem("s_const")
        s_w2 = sem("s_w2")
        s_zero = sem("s_zero")
        s_offw0 = sem("s_offw0")
        s_pad = sem("s_pad")
        s_xa = sem("s_xa")
        s_xb = sem("s_xb")
        s_tab = sem("s_tab")
        s_out = sem("s_out")
        s_patch = [sem(f"s_patch{i}") for i in range(GRING)]
        s_idx = sem("s_idx")
        s_a_tok = sem("s_a_tok")
        s_a_raw = sem("s_a_raw")
        s_a_norm = sem("s_a_norm")
        s_a_back = sem("s_a_back")
        s_a_rows = sem("s_a_rows")
        s_p_conv = sem("s_p_conv")
        s_p_shift = sem("s_p_shift")
        s_p_off = sem("s_p_off")
        s_p_po = sem("s_p_po")
        s_p_tanh = sem("s_p_tanh")
        s_p_done = sem("s_p_done")
        s_wact = sem("s_wact")
        s_first = sem("s_first")
        s_samp = sem("s_samp")
        s_trans = sem("s_trans")
        s_sampT = sem("s_sampT")
        s_low = sem("s_low")
        s_conv = sem("s_conv")
        s_x1 = sem("s_x1")
        s_z = sem("s_z")
        s_xb_used = sem("s_xb_used")
        s_zt_t = sem("s_zt_t")
        s_zt = sem("s_zt")
        s_zt_low = sem("s_zt_low")
        s_stage = [sem(f"s_stage{i}") for i in range(STAGES)]
        s_w_hi = sem("s_w_hi")
        s_w_lo = sem("s_w_lo")
        s_logit = sem("s_logit")
        s_lg = sem("s_lg")
        s_ex = sem("s_ex")
        s_comb = sem("s_comb")
        s_ct_t = sem("s_ct_t")
        s_ct = sem("s_ct")
        s_ct_low = sem("s_ct_low")
        s_h = sem("s_h")
        s_g = sem("s_g")
        s_y = sem("s_y")
        s_acc = sem("s_acc")
        s_o_t = sem("s_o_t")
        s_o = sem("s_o")
        s_var_a = sem("s_var_a")
        s_rstd_a = sem("s_rstd_a")
        s_var = sem("s_var")
        s_rstd = sem("s_rstd")
        s_ve = sem("s_ve")
        s_ve_a = sem("s_ve_a")
        s_wdve = sem("s_wdve")
        s_acc0 = sem("s_acc0")
        s_seen_dve = sem("s_seen_dve")
        s_seen_pool = sem("s_seen_pool")
        s_st_a = sem("s_st_a")
        s_place = sem("s_place")
        s_blend = sem("s_blend")
        s_fin = sem("s_fin")
        s_top = sem("s_top")
        YUSES = TILES * E

        def first_at(j):
            n = j - 4 if j >= 4 else j + PAIRS - 4
            return (n // CC, n % CC, j < 4) if n < CC * E else None

        def second_at(j):
            n = j - 6 if j >= 6 else j + PAIRS - 6
            return (n // 2, n % 2, j < 6) if n < 2 * E else None

        CHUNKS = [(conv_w[:, k], convw[0][:, k], convw[1][:, k]) for k in range(TAPS)]
        CHUNKS += [(w1[:, e], w1s[0][:, e], w1s[1][:, e]) for e in range(E)]
        CHUNKS = [tuple(ap.rearrange("p a n -> p (a n)") for ap in chunk) for chunk in CHUNKS]
        CONSTS = [(convb, conv_b.partition_broadcast(PT)), (rw_raw, router_w),
                  (b1s, b1), (tapy, tapy_c), (tapx, tapx_c),
                  (rowbase, rowbase_c), (idxbase, idxbase_c), (rev, rev_c)]
        N_CONST = len(CONSTS) + CC * 3 + 3 + TILES
        N_PAD = 4 + (FILLS if images > 1 else 0)

        last = groups + LAG_O
        cuts = sorted({0, 1, LAG_P, LAG_P + 1, LAG_X, LAG_B, LAG_M, LAG_O, LAG_O + 1, groups, groups + 1,
                       groups + LAG_P, groups + LAG_X, groups + LAG_B, groups + LAG_M, last})
        segments = [(a, b) for a, b in zip(cuts, cuts[1:])]

        def active(i):
            return {s: 0 <= i - lag < groups
                    for s, lag in (("A", 0), ("T", LAG_T), ("P", LAG_P), ("X", LAG_X), ("B", LAG_B), ("M", LAG_M), ("O", LAG_O))}

        assert (LAG_P + 1, LAG_X) in segments and LAG_X - LAG_P + 1 == FILLS

        def iterate(eng, body):
            for lo, hi in segments:
                if hi - lo == 1:
                    body(lo, active(lo))
                else:
                    with eng.Fori(lo, hi) as i:
                        body(i, active(lo))

        def count(value):
            return max(value, 0) if isinstance(value, int) else value

        def tile_of(s):
            return s // TAPS, s % TAPS

        block = ctx.enter_context(nc.Block())

        @block.sync
        def _(sp):
            def load_chunk(n):
                sp.dma_start(stage[:, n % STAGES], CHUNKS[n][0]).then_inc(s_stage[n % STAGES], 16)

            def body(i, on):
                a, x, o = i, i - LAG_X, i - LAG_O
                fills = (0, 1) if isinstance(i, int) and i == LAG_P else (i - LAG_P + 1,) \
                    if on["P"] and not on["X"] and not isinstance(i, int) else ()
                if isinstance(i, int) and i == LAG_X:
                    sp.wait_ge(s_pad, 16 * N_PAD)
                if on["A"]:
                    sp.wait_ge(s_a_tok, count(2 * a))
                    if on["O"]:
                        sp.wait_ge(s_out, 16 * o)
                    sp.dma_start(xa[:], xg[a]).then_inc(s_xa, 16)
                if isinstance(i, int) and i == 0:
                    sp.dma_start(ident[:], ident_c).then_inc(s_ident, 16)
                    sp.dma_start(inner[:], inner_c).then_inc(s_ident, 16)
                if isinstance(i, int) and i == 1:
                    for n in range(STAGES // 2):
                        load_chunk(n)
                if on["T"]:
                    d = i - LAG_T
                    sp.wait_ge(s_a_norm, d + 1)
                    entries = table.rearrange("(y x) e -> y x e", x=TW)
                    for half in range(2):
                        for r in range(2):
                            slot = d % (TABLES * GPI)
                            y = slot * ROWS + slot // GPI + (r + 1 - half)
                            dst = entries[bass.ds(y, TILES, 2), 1:HW + 1, half * C:(half + 1) * C]
                            sp.dma_start(dst.rearrange("t x c -> x t c"),
                                         xn[HW * r:HW * r + HW]).then_inc(s_tab, 16)
                if isinstance(i, int) and i == 1:
                    for n in range(STAGES // 2, STAGES):
                        load_chunk(n)
                    for dst, src in CONSTS:
                        sp.dma_start(dst[:], src).then_inc(s_const, 16)
                    sp.wait_ge(s_offw0, 1)
                    for cc in range(CC):
                        for ky in range(3):
                            sp.dma_start(offw[:, cc, ky, :, 0:OFF], off_w[:, cc, ky]).then_inc(s_const, 16)
                    for row in (0, 32, 64):
                        sp.dma_start(b2_raw[row:row + E], b2).then_inc(s_const, 16)
                    for t in range(TILES):
                        sp.dma_start(offb[:, t], off_b.partition_broadcast(PT)).then_inc(s_const, 16)
                if isinstance(i, int) and i == 2:
                    for n in range(STAGES, len(CHUNKS)):
                        sp.wait_ge(s_w_lo, n - STAGES + 1)
                        load_chunk(n)
                    sp.dma_start(w2s[:], w2).then_inc(s_w2, 16)
                    sp.wait_ge(s_zero, 1)
                    first = table[0:TH * TW].rearrange("(y x) e -> y x e", x=TW)
                    sp.dma_start(first[0, 1:HW + 1, 0:C], zeros[0:HW, 0:C]).then_inc(s_pad, 16)
                    sp.dma_start(first[HW, 1:HW + 1, C:ENT], zeros[0:HW, 0:C]).then_inc(s_pad, 16)
                    sp.dma_start(first[:, 0, :], zeros[0:TH, :]).then_inc(s_pad, 16)
                    sp.dma_start(first[:, TW - 1, :], zeros[0:TH, :]).then_inc(s_pad, 16)
                for n in fills if images > 1 else ():
                    piece = TH * TW // FILLS
                    rows = table[bass.ds(TH * TW + piece * n, piece), :]
                    sp.dma_start(rows.rearrange("(x y) e -> x y e", x=TH),
                                 zeros[0:TH].unsqueeze(1).broadcast_to([TH, piece // TH, ENT])).then_inc(s_pad, 16)
                if on["O"]:
                    sp.wait_ge(s_o, CC * o + CC)
                    sp.dma_start(out[o], outT[:]).then_inc(s_out, 16)
                if on["X"]:
                    if on["B"]:
                        sp.wait_ge(s_xb_used, x)
                    sp.dma_start(xb[:], xg[x]).then_inc(s_xb, 16)

            iterate(sp, body)
            sp.wait_ge(s_out, 16 * groups)
            sp.wait_ge(s_tab, 64 * groups)
            sp.wait_ge(s_pad, 16 * N_PAD)

        @block.gpsimd
        def _(pool):
            nc.gpsimd.memset(zeros, 0.0).then_inc(s_zero, 1)
            nc.gpsimd.memset(minus_half[:], -0.5)
            nc.gpsimd.memset(b2_raw, 0.0)
            nc.gpsimd.memset(comb[:], 0.0)
            nc.gpsimd.memset(offw[:], 0.0).then_inc(s_offw0, 1)
            nc.gpsimd.memset(shifted[:], 0.0)
            nc.gpsimd.memset(chan[:], 0.0).then_inc(s_zero, 1)

            def body(i, on):
                a, x, g, m = i, i - LAG_X, i - LAG_B, i - LAG_M

                if isinstance(i, int) and i == LAG_B:
                    pool.wait_ge(s_w_lo, len(CHUNKS))

                def rsqrt_tile(t, gg):
                    pool.wait_ge(s_var, TILES * gg + t + 1)
                    pool.wait_ge(s_z, count(TILES * gg + t))
                    pool.sem_inc(s_seen_pool, 1)
                    nc.gpsimd.tensor_scalar(ve_b[:], mv_b[:, 1:2], LN_T_EPS, None, ALU.add).then_inc(s_ve, 1)
                    pool.wait_ge(s_ve, TILES * gg + t + 1)
                    nc.gpsimd.tensor_tensor(rs_b[:], ve_b[:], minus_half[:, 0:1], ALU.pow).then_inc(s_rstd, 1)

                def rsqrt_channels():
                    pool.wait_ge(s_var_a, a + 1)
                    pool.wait_ge(s_a_norm, count(a))
                    pool.sem_inc(s_seen_pool, 1)
                    nc.gpsimd.tensor_scalar(ve_a[:], mv_a[:, :, 1], LN_C_EPS, None, ALU.add).then_inc(s_ve_a, 1)
                    pool.wait_ge(s_ve_a, a + 1)
                    nc.gpsimd.tensor_tensor(rs_a[:], ve_a[:], minus_half[:], ALU.pow).then_inc(s_rstd_a, 1)

                def keep_indices(half, gg, copies):
                    pool.wait_ge(s_p_done, gg + 1)
                    for slot in range(GRING):
                        pool.wait_ge(s_patch[slot], count(16 * (SAMP // GRING) * gg - 8 * (SAMP // GRING) * (1 - half)))
                    columns = slice(half * PAIRS, half * PAIRS + PAIRS)
                    nc.gpsimd.tensor_copy(idx[half][:], idx_ring[:, gg % RING, columns]).then_inc(s_idx, 1)
                    pool.wait_ge(s_idx, copies)

                if not on["B"]:
                    if on["M"]:
                        rsqrt_tile(TILES - 1, m)
                    if on["A"]:
                        rsqrt_channels()
                    if on["X"]:
                        keep_indices(0, x, 1)
                    return
                pool.wait_ge(s_tab, count(64 * GPI * (g // GPI) + 64 * GPI))
                for s in range(SAMP):
                    pool.wait_ge(s_pad, 16 * N_PAD)
                    pool.wait_ge(s_samp, count(SAMP * g + s - GRING + 1))
                    pool.sem_inc(s_seen_pool, 1)
                    nc.gpsimd.indirect_dma_start(
                        patch[:, s % GRING], None, table,
                        bass.IndirectOffsetOnAxis(idx[s // PAIRS][:, s % PAIRS:s % PAIRS + 1], 0)).then_inc(
                            s_patch[s % GRING], 16)
                    if s == 7:
                        if on["M"]:
                            rsqrt_tile(TILES - 1, m)
                        keep_indices(1, g, 2 * g + 2)
                    if s == 25 and on["A"]:
                        rsqrt_channels()
                    if s in (21, 27, 35):
                        rsqrt_tile((21, 27, 35).index(s), g)
                    if s == 25 and on["X"]:
                        keep_indices(0, x, 2 * x + 1)

            iterate(pool, body)

        @block.scalar
        def _(act):

            def body(i, on):
                a, p, x, g, m, o = i, i - LAG_P, i - LAG_X, i - LAG_B, i - LAG_M, i - LAG_O

                def first_corner(j):
                    for s in (2 * j, 2 * j + 1):
                        act.wait_ge(s_patch[s % GRING], 16 * (SAMP // GRING) * g + 16 * (s // GRING) + 16)
                        act.wait_ge(s_trans, count(PAIRS * g + j - SRING // 2 + 1))
                        nc.scalar.activation(samp[:, s % SRING], patch[:, s % GRING, 0:C], ACT.Copy,
                                             scale=w_act[:, s:s + 1]).then_inc(s_first, 1)

                def keep_pair(j):
                    act.wait_ge(s_trans, PAIRS * g + j + 1)
                    act.wait_ge(s_conv, count(PAIRS * g + j - TRING + 1))
                    nc.scalar.copy(sampT[0][:, j % TRING], ps_t[j % 2][:]).then_inc(s_sampT, 1)

                def gelu(e, fc, mm):
                    act.wait_ge(s_h, count(CC * E * mm + CC * e + fc + 1))
                    act.wait_ge(s_y, count(YUSES * mm + TILES * (e - 1)))
                    nc.scalar.activation(hT[:, e % 2, fc], ps_h[:], ACT.Gelu,
                                         bias=b1s[:, e, fc:fc + 1]).then_inc(s_g, 1)

                def keep_weights(half, gg, copies):
                    act.wait_ge(s_p_done, gg + 1)
                    act.wait_ge(s_first, count(SAMP * gg - PAIRS * (1 - half)))
                    columns = slice(half * PAIRS, half * PAIRS + PAIRS)
                    nc.scalar.copy(w_act[:, columns], w_ring[:, gg % RING, 0, columns]).then_inc(s_wact, 1)
                    act.wait_ge(s_wact, copies)

                if on["X"] and not on["B"]:
                    keep_weights(0, x, 1)
                if on["B"]:
                    first_corner(0)
                for j in range(PAIRS):
                    if j == 6 and on["M"]:
                        act.wait_ge(s_lg, m + 1)
                        nc.scalar.activation(ex[:], ex[:], ACT.Exp).then_inc(s_ex, 1)
                    if j == 12 and on["P"]:
                        act.wait_ge(s_p_po, p + 1)
                        act.wait_ge(s_p_done, count(p))
                        nc.scalar.activation(mask[:].rearrange("p (t k) -> p t k", t=TILES), po[:, :, 2 * TAPS:OFF],
                                             ACT.Tanh, scale=0.5).then_inc(s_p_tanh, 1)
                    if on["B"] and j + 1 < PAIRS:
                        first_corner(j + 1)
                    if on["B"]:
                        keep_pair(j)
                    if j == 4 and on["B"]:
                        keep_weights(1, g, 2 * g + 2)
                    if j == 12 and on["X"] and on["B"]:
                        keep_weights(0, x, 2 * x + 1)
                    if first_at(j) and on["O" if first_at(j)[2] else "M"]:
                        e, fc, late = first_at(j)
                        gelu(e, fc, o if late else m)
                    if j in (0, 1) and on["A"]:
                        q = j
                        act.wait_ge(s_a_tok, 2 * a + q + 1)
                        act.wait_ge(s_a_norm, count(a))
                        nc.scalar.copy(xt[:, 2 * q:2 * q + 2].rearrange("p t c -> p (t c)"),
                                       (ps_m if on["B"] else ps_conv[q])[:]).then_inc(s_a_raw, 1)
                    if j == 2 and on["M"]:
                        for cc in range(CC):
                            act.wait_ge(s_zt_t, CC * m + cc + 1)
                            act.wait_ge(s_h, count(CC * E * m))
                            nc.scalar.copy(zT[0][:, cc], (ps_h, ps_m)[cc][:]).then_inc(s_zt, 1)
                    if j in (5, 6) and on["O"]:
                        cc = j - 5
                        act.wait_ge(s_out, count(16 * o))
                        if on["A"]:
                            act.wait_ge(s_a_tok, 2 * a + 2)
                        act.wait_ge(s_o_t, CC * o + cc + 1)
                        nc.scalar.copy(outT[:, cc], ps_m[:]).then_inc(s_o, 1)
                    if j == 9 and on["P"]:
                        act.wait_ge(s_p_conv, p + 1)
                        act.wait_ge(s_p_off, count(p))
                        ps = ps_m[:].rearrange("p (r w) -> p r w", w=HW)
                        nc.scalar.copy(shifted[0:32, :, 1:HW], ps[0:32, :, 0:HW - 1])
                        nc.scalar.copy(shifted[32:64, :, :], ps[32:64, :, :])
                        nc.scalar.copy(shifted[64:96, :, 0:HW - 1], ps[64:96, :, 1:HW]).then_inc(s_p_shift, 1)
                    for q in range(2) if on["A"] and j == 11 and not on["B"] else (j - 12,) \
                            if on["A"] and j in (12, 13) and on["B"] else ():
                        act.wait_ge(s_a_back, 2 * a + q + 1)
                        if isinstance(i, int) and i == 0:
                            act.wait_ge(s_zero, 2)
                            act.wait_ge(s_ident, 32)
                        act.wait_ge(s_p_conv, count(a - 1))
                        half = (ps_m if on["B"] else ps_y[q])[:].rearrange("p (c r w) -> p c r w", c=CC, w=HW)
                        slot, row, edge = ((a - 1) % CRING, CROWS - 1, 0) if q == 0 else ((a + 1) % CRING, 0, 3)
                        nc.scalar.activation(chan[:, :, slot, row], half[:, :, edge], ACT.Copy,
                                             scale=inner[:, q, bass.ds(a, 1)])
                        nc.scalar.copy(chan[:, :, a % CRING, 1 + 4 * q:5 + 4 * q].rearrange("p c r w -> p c (r w)"),
                                       half.rearrange("p c r w -> p c (r w)")).then_inc(s_a_rows, 1)
                    if j == 12 and isinstance(i, int) and i == groups:
                        act.wait_ge(s_p_conv, groups - 1)
                        nc.scalar.mul(chan[:, :, (groups - 1) % CRING, CROWS - 1], convb[:, 0:CC * HW].rearrange(
                            "p (c w) -> p c w", c=CC), 0.0).then_inc(s_a_rows, 1)
                    if j == 14 and on["M"]:
                        act.wait_ge(s_ct_t, m + 1)
                        act.wait_ge(s_o_t, count(CC * m))
                        nc.scalar.copy(combT[:].rearrange("p t n -> p (t n)"), ps_m[0:COPIES]).then_inc(s_ct, 1)

                if isinstance(i, int) and i in (1, 2):
                    for n in range(STAGES) if i == 1 else range(STAGES, len(CHUNKS)):
                        act.wait_ge(s_stage[n % STAGES], 16 * (n // STAGES) + 16)
                        nc.scalar.copy(CHUNKS[n][1], stage[:, n % STAGES]).then_inc(s_w_hi, 1)
                    if i == 2:
                        act.wait_ge(s_const, 16 * N_CONST)
                        nc.scalar.copy(rw[:, :, 0:E], rw_raw[:]).then_inc(s_w_hi, 1)
                        nc.scalar.copy(b2s[:], b2_raw).then_inc(s_w_hi, 1)

            iterate(act, body)

        @block.vector
        def _(dve):

            def body(i, on):
                a, p, x, g, m, o = i, i - LAG_P, i - LAG_X, i - LAG_B, i - LAG_M, i - LAG_O
                def chain(semaphore, per_group, group, done=0):
                    links = [done]

                    def link(ins):
                        links[0] += 1
                        assert links[0] <= per_group
                        ins.then_inc(semaphore, 1)
                        yield
                        dve.wait_ge(semaphore, count(per_group * group + links[0]))
                    return link

                def blend(j, between):
                    pair = (2 * j, 2 * j + 1)
                    for c in range(1, 4):
                        for s in pair:
                            src = patch[:, s % GRING, c * C:(c + 1) * C]
                            if c == 1:
                                dve.wait_ge(s_patch[s % GRING], 16 * (SAMP // GRING) * g + 16 * (s // GRING) + 16)
                                dve.wait_ge(s_first, SAMP * g + s + 1)
                            else:
                                dve.wait_ge(s_blend, count(2 * SAMP * g + 4 * j + 2 * (c - 2) + (s % 2) + 1))
                            ins = nc.vector.scalar_tensor_tensor(
                                samp[:, s % SRING], src, w_dve[:, c - 1, s:s + 1], samp[:, s % SRING],
                                ALU.mult, ALU.add)
                            ins.then_inc(s_samp if c == 3 else s_blend, 1)
                            next(between, None)

                def low_parts(j):
                    dve.wait_ge(s_sampT, count(PAIRS * g + j + 1))
                    dve.wait_ge(s_conv, count(PAIRS * g + j - TRING + 1))
                    nc.vector.tensor_tensor(sampT[1][:, j % TRING], ps_t[j % 2][:],
                                            sampT[0][:, j % TRING].bitcast(F32), ALU.subtract).then_inc(s_low, 1)

                def finish_tile(t, gg):
                    dve.wait_ge(s_conv, count(PAIRS * gg + (TAPS * t + TAPS - 1) // 2 + 1))
                    ins = nc.vector.tensor_tensor(x1[:, t], ps_conv[t % 2][:, 0:C], convb[:], ALU.add)
                    ins.then_inc(s_x1, 1)
                    dve.wait_ge(s_x1, TILES * gg + t + 1)
                    nc.vector.bn_stats(st_b[:], x1[:, t]).then_inc(s_fin, 1)
                    dve.wait_ge(s_fin, TILES * gg + t + 1)
                    dve.sem_inc(s_seen_dve, 1)
                    nc.vector.bn_aggr(mv_b[:], st_b[:]).then_inc(s_var, 1)

                def norm_tile(t, gg):
                    dve.wait_ge(s_var, TILES * gg + t + 1)
                    dve.wait_ge(s_rstd, TILES * gg + t + 1)
                    dve.wait_ge(s_zt_t, count(CC * gg))
                    nc.vector.tensor_scalar(z[:, t], x1[:, t], mv_b[:, 0:1], rs_b[:], ALU.subtract,
                                            ALU.mult).then_inc(s_z, 1)

                def add_expert(e, half, mm):
                    for t in (2 * half, 2 * half + 1):
                        use = TILES * e + t
                        dve.wait_ge(s_y, count(YUSES * mm + use + 1))
                        dve.wait_ge(s_acc, count(YUSES * mm + use - TILES + 1))
                        nc.vector.scalar_tensor_tensor(acc[:, t], ps_y[use % 2][:, 0:C], comb[:, t, e:e + 1], acc[:, t],
                                                       ALU.mult, ALU.add).then_inc(s_acc, 1)

                def channel_stats():
                    dve.wait_ge(s_a_raw, 2 * a + 2)
                    for t in range(TILES):
                        ins = nc.vector.bn_stats(st_a[:, t], xt[:, t])
                    ins.then_inc(s_st_a, 1)
                    dve.wait_ge(s_st_a, a + 1)
                    dve.sem_inc(s_seen_dve, 1)
                    for t in range(TILES):
                        ins = nc.vector.bn_aggr(mv_a[:, t], st_a[:, t])
                    ins.then_inc(s_var_a, 1)

                def norm_channels():
                    dve.wait_ge(s_var_a, a + 1)
                    dve.wait_ge(s_rstd_a, a + 1)
                    dve.wait_ge(s_tab, count(64 * a))
                    dve.wait_ge(s_a_back, count(2 * a))
                    for t in range(TILES):
                        ins = nc.vector.tensor_scalar(xn[:, t], xt[:, t], mv_a[:, t, 0:1], rs_a[:, t:t + 1],
                                                      ALU.subtract, ALU.mult)
                    ins.then_inc(s_a_norm, 1)

                def over_experts(r):
                    return red[:, r].unsqueeze(2).broadcast_to([PT, TILES, E])

                def take_logits():
                    then = chain(s_top, 21, m)
                    dve.wait_ge(s_logit, m + 1)
                    dve.wait_ge(s_acc, count(YUSES * m))
                    parts = ps_m[:, 0:2 * TILES * E].rearrange("p (t n e) -> p t n e", n=2, e=E)
                    yield from then(nc.vector.tensor_copy(lg[:], parts[:, :, 1]))
                    yield from then(nc.vector.tensor_tensor(lg[:], parts[:, :, 0], lg[:], ALU.add))
                    yield from then(nc.vector.tensor_reduce(red[:, 0], lg[:], AX, ALU.max))
                    nc.vector.tensor_tensor(ex[:], lg[:], over_experts(0), ALU.subtract).then_inc(s_lg, 1)

                def top2():
                    then = chain(s_top, 21, m, 3)
                    yield from then(nc.vector.tensor_tensor(cand[:], lg[:], over_experts(0), ALU.is_equal))
                    yield from then(nc.vector.tensor_tensor(cand[:], cand[:], rev[:], ALU.mult))
                    yield from then(nc.vector.tensor_reduce(red[:, 1], cand[:], AX, ALU.max))
                    yield from then(nc.vector.tensor_tensor(hot1[:], cand[:], over_experts(1), ALU.is_equal))
                    yield from then(nc.vector.scalar_tensor_tensor(lg2[:], hot1[:], -3.0e38, lg[:], ALU.mult, ALU.add))
                    yield from then(nc.vector.tensor_reduce(red[:, 1], lg2[:], AX, ALU.max))
                    yield from then(nc.vector.tensor_tensor(cand[:], lg2[:], over_experts(1), ALU.is_equal))
                    yield from then(nc.vector.tensor_tensor(cand[:], cand[:], rev[:], ALU.mult))
                    yield from then(nc.vector.tensor_reduce(red[:, 1], cand[:], AX, ALU.max))
                    yield from then(nc.vector.tensor_tensor(hot2[:], cand[:], over_experts(1), ALU.is_equal))
                    yield from then(nc.vector.tensor_tensor(hot1[:], hot1[:], hot2[:], ALU.add))

                def combine_weights():
                    then = chain(s_top, 21, m, 14)
                    dve.wait_ge(s_ex, m + 1)
                    yield from then(nc.vector.tensor_reduce(red[:, 2], ex[:], AX, ALU.add))
                    yield from then(nc.vector.reciprocal(red[:, 2], red[:, 2]))
                    yield from then(nc.vector.tensor_tensor(ex[:], ex[:], over_experts(2), ALU.mult))
                    yield from then(nc.vector.tensor_tensor(ex[:], ex[:], hot1[:], ALU.mult))
                    yield from then(nc.vector.tensor_reduce(red[:, 3], ex[:], AX, ALU.add))
                    yield from then(nc.vector.tensor_scalar(red[:, 3], red[:, 3], 1e-12, None, ALU.max))
                    yield from then(nc.vector.reciprocal(red[:, 3], red[:, 3]))
                    if isinstance(m, int) and m == 0:
                        dve.wait_ge(s_zero, 2)
                    for row in (64, 32, 0):
                        ins = nc.vector.tensor_tensor(comb[:, :, row:row + E], ex[:], over_experts(3), ALU.mult)
                    ins.then_inc(s_comb, 1)
                    dve.wait_ge(s_comb, m + 1)

                def take_offsets():
                    then = chain(s_place, 14, p)
                    if isinstance(i, int) and i == LAG_P:
                        dve.wait_ge(s_const, 16 * N_CONST)
                    dve.wait_ge(s_p_off, p + 1)
                    dve.wait_ge(s_p_tanh, count(p))
                    parts = ps_m[:, 0:TILES * 96].rearrange("p (t x k) -> p t x k", x=3, k=32)
                    yield from then(nc.vector.tensor_tensor(po[:], parts[:, :, 0, 0:OFF], offb[:], ALU.add))
                    yield from then(nc.vector.tensor_tensor(po[:], parts[:, :, 1, 0:OFF], po[:], ALU.add))
                    nc.vector.tensor_tensor(po[:], parts[:, :, 2, 0:OFF], po[:], ALU.add).then_inc(s_p_po, 1)
                    dve.wait_ge(s_p_po, p + 1)

                def tk(ap):
                    return ap.rearrange("p (t k) -> p t k", t=TILES)

                def place_samples():
                    then = chain(s_place, 14, p, 2)
                    nc.vector.scalar_tensor_tensor(tk(pos[:, 0]), tk(tapy[:]), rowbase[:, bass.ds(p, 1)],
                                                   po[:, :, 0:2 * TAPS:2], ALU.add, ALU.add)
                    yield from then(nc.vector.tensor_tensor(tk(pos[:, 1]), tk(tapx[:]), po[:, :, 1:2 * TAPS:2], ALU.add))
                    yield from then(nc.vector.tensor_scalar(pos[:], pos[:], -1.0, float(HW), ALU.max, ALU.min))
                    yield from then(nc.vector.tensor_copy(cell_i[:], pos[:]))
                    yield from then(nc.vector.tensor_copy(cell[:], cell_i[:]))
                    yield from then(nc.vector.tensor_tensor(over[:], cell[:], pos[:], ALU.is_gt))
                    yield from then(nc.vector.tensor_tensor(cell[:], cell[:], over[:], ALU.subtract))
                    yield from then(nc.vector.tensor_scalar(cell[:], cell[:], float(HW - 1), None, ALU.min))
                    yield from then(nc.vector.tensor_tensor(hi_w[:], pos[:], cell[:], ALU.subtract))
                    yield from then(nc.vector.tensor_scalar(lo_w[:], hi_w[:], -1.0, 1.0, ALU.mult, ALU.add))

                def place_weights():
                    then = chain(s_place, 14, p, 11)
                    dve.wait_ge(s_p_tanh, p + 1)
                    yield from then(nc.vector.tensor_scalar(mask[:], mask[:], 0.5, 0.5, ALU.mult, ALU.add))
                    nc.vector.tensor_tensor(my[:, 0], lo_w[:, 0], mask[:], ALU.mult)
                    yield from then(nc.vector.tensor_tensor(my[:, 1], hi_w[:, 0], mask[:], ALU.mult))
                    yield from then(nc.vector.scalar_tensor_tensor(flat[:], cell[:, 0], float(TW), cell[:, 1], ALU.mult, ALU.add))
                    for c in range(4):
                        nc.vector.tensor_tensor(w_ring[:, p % RING, c], my[:, c % 2],
                                                (lo_w if c < 2 else hi_w)[:, 1], ALU.mult)
                    nc.vector.tensor_scalar(idx_ring[:, p % RING], flat[:], idxbase[:, bass.ds(p, 1)], None,
                                            ALU.add).then_inc(s_p_done, 1)

                def keep_weights(half, gg, copies):
                    dve.wait_ge(s_p_done, gg + 1)
                    dve.wait_ge(s_samp, count(SAMP * gg - PAIRS * (1 - half)))
                    columns = slice(half * PAIRS, half * PAIRS + PAIRS)
                    nc.vector.tensor_copy(w_dve[:, :, columns], w_ring[:, gg % RING, 1:4, columns]).then_inc(s_wdve, 1)
                    dve.wait_ge(s_wdve, copies)

                if on["X"] and not on["B"]:
                    keep_weights(0, x, 1)
                if isinstance(i, int) and i == LAG_B:
                    dve.wait_ge(s_w_lo, len(CHUNKS) + 2)
                for j in range(PAIRS):
                    between = iter(())
                    if j == 6 and on["M"]:
                        between = top2()
                    if j == 7 and on["M"]:
                        between = combine_weights()
                    if j == 13 and on["P"]:
                        between = place_samples()
                    if j == 14 and on["P"]:
                        between = place_weights()
                    if on["B"]:
                        blend(j, between)
                        if j:
                            low_parts(j - 1)
                    for _ in between:
                        pass
                    if j == 4 and on["B"]:
                        keep_weights(1, g, 2 * g + 2)
                    if j == 12 and on["X"] and on["B"]:
                        keep_weights(0, x, 2 * x + 1)
                    if j == 0 and on["O"]:
                        add_expert(*second_at(PAIRS - 1)[:2], o)
                    if j == 7 and on["M"]:
                        dve.wait_ge(s_o_t, count(CC * m))
                        dve.wait_ge(s_z, TILES * m + TILES)
                        nc.vector.tensor_tensor(acc[:], x1[:], z[:], ALU.add).then_inc(s_acc0, 1)
                        dve.wait_ge(s_acc0, m + 1)
                    if j and second_at(j - 1) and on["O" if second_at(j - 1)[2] else "M"]:
                        e, half, late = second_at(j - 1)
                        add_expert(e, half, o if late else m)
                    if j == 1 and on["M"]:
                        finish_tile(TILES - 1, m)
                    if j == 2 and on["M"]:
                        norm_tile(TILES - 1, m)
                    if j == 3 and on["M"]:
                        for cc in range(CC):
                            dve.wait_ge(s_zt, CC * m + cc + 1)
                            dve.wait_ge(s_h, count(CC * E * m))
                            nc.vector.tensor_tensor(zT[1][:, cc], (ps_h, ps_m)[cc][:], zT[0][:, cc].bitcast(F32),
                                                    ALU.subtract).then_inc(s_zt_low, 1)
                    if j == 5 and on["M"]:
                        for _ in take_logits():
                            pass
                    if on["B"] and j in (8, 11, 16):
                        finish_tile((8, 11, 16).index(j), g)
                    if on["B"] and j in (9, 14, 17):
                        norm_tile((9, 14, 17).index(j), g)
                    if j == 9 and on["A"]:
                        channel_stats()
                    if j == 10 and on["A"]:
                        norm_channels()
                    if j == 11 and on["P"]:
                        for _ in take_offsets():
                            pass
                    if j == 15 and on["M"]:
                        dve.wait_ge(s_ct, m + 1)
                        last_copy = combT[64:64 + E].rearrange("p t n -> p (t n)")
                        nc.vector.tensor_tensor(last_copy, ps_m[64:64 + E], last_copy.bitcast(F32),
                                                ALU.subtract).then_inc(s_ct_low, 1)
                if on["B"]:
                    low_parts(PAIRS - 1)

                if isinstance(i, int) and i in (1, 2):
                    for n in range(STAGES) if i == 1 else range(STAGES, len(CHUNKS)):
                        dve.wait_ge(s_w_hi, n + 1)
                        nc.vector.tensor_tensor(CHUNKS[n][2], stage[:, n % STAGES], CHUNKS[n][1].bitcast(F32),
                                                ALU.subtract).then_inc(s_w_lo, 1)
                    if i == 2:
                        dve.wait_ge(s_w_hi, len(CHUNKS) + 2)
                        nc.vector.tensor_tensor(b2s[32:32 + E], b2_raw[32:32 + E], b2s[32:32 + E].bitcast(F32),
                                                ALU.subtract).then_inc(s_w_lo, 1)
                        nc.vector.tensor_tensor(rw[:, :, E:2 * E], rw_raw[:], rw[:, :, 0:E].bitcast(F32),
                                                ALU.subtract).then_inc(s_w_lo, 1)

            iterate(dve, body)

        @block.tensor
        def _(pe):
            pe.wait_ge(s_ident, 32)
            PARTS = ((0, 0), (0, 1), (1, 0))

            def body(i, on):
                a, p, g, m, o = i, i - LAG_P, i - LAG_B, i - LAG_M, i - LAG_O

                if isinstance(i, int) and i == LAG_B:
                    pe.wait_ge(s_w_lo, len(CHUNKS) + 2)
                    pe.wait_ge(s_w2, 16)

                def transpose_pair(j):
                    pe.wait_ge(s_samp, SAMP * g + 2 * j + 2)
                    pe.wait_ge(s_low, count(PAIRS * g + j - 1))
                    for h in range(2):
                        for cc in range(CC):
                            ins = nc.tensor.transpose(ps_t[j % 2][:, h, cc],
                                                      samp[:, (2 * j + h) % SRING, cc * PT:(cc + 1) * PT], ident[:])
                    ins.then_inc(s_trans, 1)

                def convolve_pair(j):
                    pe.wait_ge(s_low, PAIRS * g + j + 1)
                    for h in range(2):
                        t, k = tile_of(2 * j + h)
                        dst = ps_conv[t % 2][:, 0:C]
                        if k == 0:
                            pe.wait_ge(s_x1, count(TILES * g + t - 1))
                            if isinstance(g, int) and g == 0:
                                pe.wait_ge(s_a_raw, 2 * LAG_B)
                            if t == 0:
                                pe.wait_ge(s_xb, 16 * g + 16)
                            for cc in range(CC):
                                ins = nc.tensor.matmul(dst[:, cc * PT:(cc + 1) * PT], xb[:, cc, t * PT:(t + 1) * PT],
                                                       ident[:], start=(cc == 0), stop=False, is_transpose=True,
                                                       skip_group_check=True)
                            if t == TILES - 1:
                                ins.then_inc(s_xb_used, 1)
                        for cc in range(CC):
                            for n, (x, w) in enumerate(PARTS):
                                ins = nc.tensor.matmul(dst, sampT[x][:, j % TRING, h, cc], convw[w][:, k, cc],
                                                       start=False, stop=(k == TAPS - 1 and cc == CC - 1 and n == 2),
                                                       skip_group_check=True)
                    ins.then_inc(s_conv, 1)

                def first_product(e, fc, mm):
                    pe.wait_ge(s_g, count(CC * E * mm + CC * e + fc))
                    pe.wait_ge(s_zt_low, CC * mm + CC)
                    for cc in range(CC):
                        for n, (x, w) in enumerate(PARTS):
                            ins = nc.tensor.matmul(ps_h[:], w1s[w][:, e, cc, fc * PT:(fc + 1) * PT], zT[x][:, cc],
                                                   start=(cc == 0 and n == 0), stop=(cc == CC - 1 and n == 2))
                    ins.then_inc(s_h, 1)

                def second_product(e, half, mm):
                    pe.wait_ge(s_g, CC * E * mm + CC * e + CC)
                    for t in (2 * half, 2 * half + 1):
                        use = TILES * e + t
                        pe.wait_ge(s_acc, count(YUSES * mm + use - 1))
                        for fc in range(CC):
                            ins = nc.tensor.matmul(ps_y[use % 2][:, 0:C], hT[:, e % 2, fc, t * PT:(t + 1) * PT],
                                                   w2s[:, e, fc], start=(fc == 0), stop=(fc == CC - 1))
                        ins.then_inc(s_y, 1)

                def misc_bank_free():
                    if on["M"]:
                        pe.wait_ge(s_ct_low, count(m))
                    elif on["O"]:
                        pe.wait_ge(s_ct_low, groups)
                    if on["P"]:
                        pe.wait_ge(s_p_po, count(p))
                    if on["P"] or on["A"]:
                        pe.wait_ge(s_a_rows, count(2 * a) if on["A"] else 2 * groups)

                for j in range(PAIRS):
                    if on["B"]:
                        transpose_pair(j)
                    if first_at(j) and on["O" if first_at(j)[2] else "M"]:
                        e, fc, late = first_at(j)
                        first_product(e, fc, o if late else m)
                    if second_at(j) and on["O" if second_at(j)[2] else "M"]:
                        e, half, late = second_at(j)
                        second_product(e, half, o if late else m)
                    if j in (0, 1) and on["A"]:
                        q = j
                        pe.wait_ge(s_xa, 16 * a + 16)
                        if on["B"]:
                            misc_bank_free()
                        pe.wait_ge(s_a_raw, count(2 * a + q - (0 if on["B"] else 1)))
                        for t in (2 * q, 2 * q + 1):
                            for cc in range(CC):
                                col = (t % 2) * C + cc * PT
                                ins = nc.tensor.transpose((ps_m if on["B"] else ps_conv[q])[:, col:col + PT],
                                                          xa[:, cc, t * PT:(t + 1) * PT], ident[:])
                        ins.then_inc(s_a_tok, 1)
                    if j == 2 and on["M"]:
                        pe.wait_ge(s_z, TILES * m + TILES)
                        pe.wait_ge(s_g, count(CC * E * m))
                        misc_bank_free()
                        if on["A"]:
                            pe.wait_ge(s_a_raw, 2 * a + 2)
                        for cc in range(CC):
                            for t in range(TILES):
                                ins = nc.tensor.transpose((ps_h, ps_m)[cc][:, t * PT:(t + 1) * PT],
                                                          z[:, t, cc * PT:(cc + 1) * PT], ident[:])
                            ins.then_inc(s_zt_t, 1)
                    if j == 4 and on["M"]:
                        pe.wait_ge(s_zt_low, CC * m + CC)
                        for t in range(TILES):
                            for cc in range(CC):
                                tile = slice(t * PT, (t + 1) * PT)
                                nc.tensor.matmul(ps_m[:, 2 * t * E:2 * (t + 1) * E], zT[0][:, cc, tile], rw[:, cc],
                                                 start=(cc == 0), stop=False, skip_group_check=True)
                                ins = nc.tensor.matmul(ps_m[:, 2 * t * E:(2 * t + 1) * E], zT[1][:, cc, tile],
                                                       rw[:, cc, 0:E], start=False, stop=(cc == CC - 1),
                                                       skip_group_check=True)
                        ins.then_inc(s_logit, 1)
                    if j in (5, 6) and on["O"]:
                        cc = j - 5
                        pe.wait_ge(s_acc, YUSES * o + YUSES)
                        misc_bank_free()
                        if on["A"]:
                            pe.wait_ge(s_a_raw, 2 * a + 2)
                        if on["M"]:
                            pe.wait_ge(s_lg, m + 1)
                        pe.wait_ge(s_o, count(CC * o + cc))
                        for t in range(TILES):
                            nc.tensor.matmul(ps_m[:, t * PT:(t + 1) * PT], acc[:, t, cc * PT:(cc + 1) * PT],
                                             ident[:], start=(t == 0), stop=False, is_transpose=True,
                                             skip_group_check=True)
                        ins = nc.tensor.matmul(ps_m[:], b2s[:, cc * PT:(cc + 1) * PT],
                                               combT[:].rearrange("p t n -> p (t n)"), start=False, stop=True,
                                               skip_group_check=True)
                        ins.then_inc(s_o_t, 1)
                    if j in (7, 8) and on["P"]:
                        if isinstance(i, int) and i == LAG_P:
                            pe.wait_ge(s_const, 16 * N_CONST)
                            pe.wait_ge(s_zero, 2)
                        pe.wait_ge(s_a_rows, 2 * (p + 2) if not isinstance(i, int) or p < groups - 1 else 2 * groups + 1)
                        misc_bank_free()
                        if on["A"] and on["B"]:
                            pe.wait_ge(s_a_raw, 2 * a + 2)
                        if on["O"]:
                            pe.wait_ge(s_o, CC * o + CC)
                        for n, (ky, cc) in enumerate((ky, cc) for ky in range(3) for cc in range(CC)):
                            if n // 3 == j - 7:
                                src = chan[:, cc, p % CRING, ky:ky + ROWS].rearrange("p r w -> p (r w)")
                                ins = nc.tensor.matmul(ps_m[0:96], offw[:, cc, ky].rearrange("p x o -> p (x o)"), src,
                                                       start=(n == 0), stop=(n == 5))
                        if j == 8:
                            ins.then_inc(s_p_conv, 1)
                    if j == 10 and on["P"]:
                        pe.wait_ge(s_p_shift, p + 1)
                        for t in range(TILES):
                            lhs = shifted[:, 2 * t:2 * t + 2, :].rearrange("p r w -> p (r w)")
                            ins = nc.tensor.transpose(ps_m[:, t * 96:(t + 1) * 96], lhs, ident[0:96, 0:96])
                        ins.then_inc(s_p_off, 1)
                    for q in range(2) if on["A"] and j == 11 and not on["B"] else (j - 12,) \
                            if on["A"] and j in (12, 13) and on["B"] else ():
                        pe.wait_ge(s_a_norm, a + 1)
                        if on["B"]:
                            pe.wait_ge(s_p_po, p + 1)
                        if on["O"]:
                            pe.wait_ge(s_o, CC * o + CC)
                        pe.wait_ge(s_a_rows, count(2 * a + q - (0 if on["B"] else 1)))
                        for t in (2 * q, 2 * q + 1):
                            for cc in range(CC):
                                col = cc * 2 * PT + (t % 2) * PT
                                ins = nc.tensor.transpose((ps_m if on["B"] else ps_y[q])[:, col:col + PT],
                                                          xn[:, t, cc * PT:(cc + 1) * PT], ident[:])
                        ins.then_inc(s_a_back, 1)
                    if j == 14 and on["M"]:
                        pe.wait_ge(s_comb, m + 1)
                        if on["P"]:
                            pe.wait_ge(s_p_po, p + 1)
                        if on["A"]:
                            pe.wait_ge(s_a_rows, 2 * a + 2)
                        if on["O"]:
                            pe.wait_ge(s_o, CC * o + CC)
                        for t in range(TILES):
                            ins = nc.tensor.transpose(ps_m[0:COPIES, t * PT:(t + 1) * PT], comb[:, t], ident[:])
                        ins.then_inc(s_ct_t, 1)
                    if on["B"] and j:
                        convolve_pair(j - 1)
                if on["B"]:
                    convolve_pair(PAIRS - 1)

            iterate(pe, body)


def run_inputs(np, x, L0_conv_weight, L0_conv_bias, L0_conv_p_weight, L0_conv_p_bias,
               L0_ffn_router_w, L0_ffn_w1, L0_ffn_b1, L0_ffn_w2, L0_ffn_b2):
    groups = x.shape[0] * GPI
    p = np.arange(PT)
    t, k = np.arange(SAMP) // TAPS, np.arange(SAMP) % TAPS
    g = np.arange(groups)
    f32 = np.float32
    every = np.ones((PT, 1), f32)
    arrays = {
        "xg": x.reshape(-1, CC, PT, GPI, GT).transpose(0, 3, 2, 1, 4).reshape(groups, PT, CC, GT),
        "conv_w": L0_conv_weight.reshape(C, CC, PT, TAPS).transpose(2, 3, 1, 0),
        "conv_b": L0_conv_bias,
        "off_w": L0_conv_p_weight.reshape(OFF, CC, PT, 3, 3).transpose(2, 1, 3, 4, 0),
        "off_b": L0_conv_p_bias.reshape(OFF),
        "router_w": L0_ffn_router_w.reshape(E, CC, PT).transpose(2, 1, 0),
        "w1": L0_ffn_w1.reshape(E, CC, PT, C).transpose(2, 0, 1, 3),
        "b1": L0_ffn_b1.reshape(E, CC, PT).transpose(2, 0, 1),
        "w2": L0_ffn_w2.reshape(E, CC, PT, C).transpose(2, 0, 1, 3),
        "b2": L0_ffn_b2,
        "ident_c": np.eye(PT, dtype=f32),
        "tapy_c": every * (2 * t + k // 3).astype(f32),
        "tapx_c": (p[:, None] % HW + k % 3 - 1).astype(f32),
        "rowbase_c": ((g % GPI) * ROWS + p[:, None] // HW - 1).astype(f32),
        "idxbase_c": every * ((g // GPI % TABLES) * (TH * TW) + TW + 1).astype(f32),
        "inner_c": (every[:, :, None] * np.stack([g % GPI != 0, g % GPI != GPI - 1])).astype(f32),
        "rev_c": np.ones((PT, TILES, 1), f32) * (E - np.arange(E)).astype(f32),
    }
    return groups, {n: np.ascontiguousarray(a) for n, a in arrays.items()}


def kernel(**inputs):
    import numpy as np
    import concourse.bacc as bacc
    from concourse.bass_utils import run_bass_kernel_spmd

    groups, arrays = run_inputs(np, **{n: np.asarray(a) for n, a in inputs.items()})
    nc = bacc.Bacc("TRN2", target_bir_lowering=False, num_devices=1)
    args = [nc.dram_tensor(n, a.shape, mybir.dt.from_np(a.dtype), kind="ExternalInput").ap()
            for n, a in arrays.items()]
    out = nc.dram_tensor("out", (groups, PT, CC, GT), F32, kind="ExternalOutput").ap()
    build(nc, groups, *args, out)
    r = run_bass_kernel_spmd(nc, [arrays], core_ids=[0]).results[0]["out"]
    return r.reshape(-1, GPI, PT, CC, GT).transpose(0, 3, 2, 1, 4).reshape(inputs["x"].shape)
```
